# Optimizing a Trainium2 kernel written in Bass

```python
import numpy as np
import jax
import jax.numpy as jnp

def _softmax(x, axis=-1):
    return jax.nn.softmax(x, axis=axis)

def _gelu(x):
    return jax.nn.gelu(x, approximate=True)

def _silu(x):
    return jax.nn.silu(x)

def _sigmoid(x):
    return jax.nn.sigmoid(x)

def _layernorm(x, axis=-1, eps=1e-05):
    m = jnp.mean(x, axis=axis, keepdims=True)
    v = jnp.var(x, axis=axis, keepdims=True)
    return (x - m) / jnp.sqrt(v + eps)

def _scatter_add(tgt, idx, src, axis=0):
    return tgt.at[idx].add(src)

def _segment_sum(src, seg, n):
    return jax.ops.segment_sum(src, seg, n)
kernel_name = 'mk_gnn_resnorm_d1_gnn_r8_8fd6c6'

def setup_inputs(seed: int=0):
    np.random.seed(seed)
    _w = jnp.asarray

    def _rec_inputs():
        import jax
        import jax.numpy as jnp
        _gk = jax.random.key(seed)
        x = -0.0005207 + 1.001 * jax.random.normal(jax.random.fold_in(_gk, 1), (6250, 128), jnp.float32)
        src = jax.random.randint(jax.random.fold_in(_gk, 2), (100000,), 0, 6250, jnp.int32)
        dst = jnp.minimum((6250 * jax.random.uniform(jax.random.fold_in(_gk, 3), (100000,)) ** 2.0).astype(jnp.int32), 49999)
        _o = jnp.argsort(dst, stable=True)
        src = src[_o]
        dst = dst[_o]
        edge_type_50 = jax.random.randint(jax.random.fold_in(_gk, 12), (100000,), 0, 50, jnp.int32)
        return (x, src, dst, edge_type_50)
    x, src, dst, edge_type_50 = _rec_inputs()

    def _L0_gnn_setup():
        import jax, jax.numpy as jnp
        import numpy as np
        N_ENT = 2048
        N_REL = 50
        D = 128
        B = 4
        E = 32768
        key = jax.random.key(seed)
        k1, k2, k3, k4, k5, k6 = jax.random.split(key, 6)
        x = jax.random.normal(k1, (N_ENT, D), dtype=jnp.float32)
        bases = jax.random.normal(k2, (B, D, D), dtype=jnp.float32) * 0.05
        comps = jax.random.normal(k3, (N_REL, B), dtype=jnp.float32)
        alpha = jax.random.normal(k4, (N_REL, 1), dtype=jnp.float32)
        edge_index = jax.random.randint(k5, (2, E), 0, N_ENT, dtype=jnp.int64)
        edge_type = jax.random.randint(k6, (E,), 0, N_REL, dtype=jnp.int64)
        return {'x': x, 'bases': bases, 'comps': comps, 'alpha': alpha, 'edge_index': edge_index, 'edge_type': edge_type}
    _L0_gnn_all = _L0_gnn_setup()
    _L0_gnn_in = {k: v for k, v in _L0_gnn_all.items() if k in ('bases', 'comps', 'alpha')}
    del _L0_gnn_all
    return {'x': x, 'src': src, 'dst': dst, 'edge_type_50': edge_type_50, 'L0_gnn_bases': _L0_gnn_in['bases'], 'L0_gnn_comps': _L0_gnn_in['comps'], 'L0_gnn_alpha': _L0_gnn_in['alpha']}

def reference(x, src, dst, edge_type_50, L0_gnn_bases, L0_gnn_comps, L0_gnn_alpha):
    import jax
    import jax.numpy as jnp

    def _L0_gnn_ref(x, bases, comps, alpha, edge_index, edge_type):
        import jax, jax.numpy as jnp
        import numpy as np
        N_ENT = 2048
        N_REL = 50
        D = 128
        B = 4
        E = 32768
        n = x.shape[0]
        row, col = (edge_index[0], edge_index[1])
        ones = jnp.ones(row.shape, x.dtype)
        deg = jax.ops.segment_sum(ones, row, num_segments=n)
        deg_inv = jnp.where(deg > 0, jax.lax.rsqrt(jnp.maximum(deg, 1.0)), 0.0)
        norm = deg_inv[row] * deg_inv[col]
        h_j = x[col]
        c_e = comps[edge_type]
        hj_b = c_e[:, :, None] * h_j[:, None, :]
        msg = jnp.einsum('ebd,bdf->ef', hj_b, bases)
        msg = msg * alpha[edge_type] * norm[:, None]
        out = jax.ops.segment_sum(msg, row, num_segments=n)
        return out
    edge_index = jnp.stack([src, dst])
    x = _layernorm(x + _L0_gnn_ref(x, L0_gnn_bases, L0_gnn_comps, L0_gnn_alpha, edge_index, edge_type_50), axis=-1)
    return x

_drawn_inputs = setup_inputs


def setup_inputs(seed=0):
    import zlib

    import numpy as np

    out = dict(_drawn_inputs(seed))
    spreads = {}
    factors = {}
    for name, (base, spread) in spreads.items():
        noise = np.random.default_rng([zlib.crc32(name.encode()), seed]).standard_normal(out[name].shape)
        drawn = base * np.exp(spread * noise) if base else spread * noise
        out[name] = jnp.asarray(drawn.astype(out[name].dtype))
    for name, factor in factors.items():
        out[name] = (out[name] * factor).astype(out[name].dtype)
    return out
```

```python
from contextlib import ExitStack

import concourse.bass as bass
from concourse import mybir

ALU = mybir.AluOpType
ACT = mybir.ActivationFunctionType
AX = mybir.AxisListType
F32 = mybir.dt.float32
BF16 = mybir.dt.bfloat16
I32 = mybir.dt.int32

P = 128
GROUPS = 4
BODIES = 25
SRC_U = 8
TILE_U = 10
HALF = TILE_U // 2
LAG = 3
SRC_AT = [1, 2, 4, 5, 7, 8, 10, 11]
MARK = 0x2000
LOW13 = MARK - 1


def relational_layer(nc, x, src, dst, etype, bases, comps, alpha, out):
    N, D = x.shape
    E = src.shape[0]
    NBASE = bases.shape[0]
    NREL = comps.shape[0]
    ZW = NBASE * D
    NB = (N + P - 1) // P
    TAIL = N - (NB - 1) * P
    COLS = (E + P - 1) // P
    LASTC = E - (P - 1) * COLS
    SRC_G = BODIES * SRC_U
    TILES = BODIES * TILE_U
    ALLC = GROUPS * SRC_G
    PAIRS = TILES // 2
    assert D == P and N <= MARK and NREL <= 64 and NB <= 63
    assert ALLC >= COLS and 2 * TILES <= 512
    assert (SRC_G * P + NB * (P - 1)) // P <= TILES

    with ExitStack() as ctx:
        def sb(name, shape, dt):
            return ctx.enter_context(nc.sbuf_tensor(name, shape, dt))

        def sem(name):
            return ctx.enter_context(nc.semaphore(name))

        z_table = nc.dram_tensor("z_table", (NB * P, ZW), F32).ap()
        type_rows = nc.dram_tensor("type_rows", (2, PAIRS, P), BF16).ap()

        block_sum = sb("block_sum", [P, 64 * D], F32)
        x_sb = sb("x_sb", [P, NB, D], F32)
        big = sb("big", [P, SRC_G * NB], F32)
        slot_scan = big[:, :]
        type_hot = big[:, 0:PAIRS * P // 2].bitcast(BF16)
        work = sb("work", [P, TILE_U * (NBASE + 1) * D], F32)
        hot_blk = work[:, 0:SRC_G * NB // 2].bitcast(BF16)
        lo0 = SRC_G * NB // 2
        hot_low = work[:, lo0:lo0 + SRC_U * P].bitcast(BF16)
        y_ring = work[:, 0:7 * D]
        yt_ring = work[:, 7 * D:14 * D]
        wb = work[:, 0:TILE_U * NBASE * D]
        hot_row = work[:, TILE_U * NBASE * D:]
        z_ring = sb("z_ring", [P, TILE_U, ZW], F32)
        src_i = sb("src_i", [P, ALLC], I32)
        dst_i = sb("dst_i", [P, ALLC], I32)
        typ_i = sb("typ_i", [P, ALLC], I32)
        hi_b = sb("hi_b", [P, ALLC], BF16)
        lo_b = sb("lo_b", [P, ALLC], BF16)
        hi_g = sb("hi_g", [P, SRC_G], BF16)
        lo_g = sb("lo_g", [P, SRC_G], BF16)
        records = sb("records", [P, ALLC // SRC_U, 3, SRC_U], F32)
        idx_all = sb("idx_all", [P, TILES + TILE_U], I32)
        row_all = sb("row_all", [P, TILES], F32)
        w_all = sb("w_all", [P, TILES * NBASE], F32)
        tmp_a = sb("tmp_a", [P, 256], I32)
        tmp_b = sb("tmp_b", [P, 256], I32)
        type_b = sb("type_b", [P, TILES], BF16)
        type_t = sb("type_t", [P, 2, P], BF16)
        block_words = sb("block_words", [1, GROUPS * 2 * BODIES], I32)
        words_g = sb("words_g", [1, 2 * BODIES], I32)
        blk_i = sb("blk_i", [1, TILES], I32)
        hot_slot = sb("hot_slot", [P, SRC_U, P], BF16)
        hot_tile = sb("hot_tile", [P, SRC_U, TILES], F32)
        src_now = sb("src_now", [P, 3, SRC_U], F32)
        row_now = sb("row_now", [P, TILE_U], F32)
        w0_now = sb("w0_now", [P, TILE_U * NBASE], F32)
        w_now = sb("w_now", [P, TILE_U * NBASE], F32)
        idx_now = sb("idx_now", [P, TILE_U], I32)
        bases_sb = sb("bases_sb", [P, NBASE, D], F32)
        iota_i = sb("iota_i", [P, 256], I32)
        pcol_i = sb("pcol_i", [P, 2], I32)
        pcol = sb("pcol", [P, 2], F32)
        iota_f = sb("iota_f", [P, 256], F32)
        iota_b = sb("iota_b", [P, P], BF16)
        iota_mark = sb("iota_mark", [P, P], BF16)
        ident_f = sb("ident_f", [P, P], F32)
        ident_b = sb("ident_b", [P, P], BF16)
        below = sb("below", [P, P], BF16)
        ones_b = sb("ones_b", [P, SRC_G], BF16)
        zeros_b = sb("zeros_b", [P, 512], BF16)
        w_table = sb("w_table", [P, 2 * NBASE], F32)
        w_rest = sb("w_rest", [P, 2 * NBASE], F32)
        alpha_sb = sb("alpha_sb", [P, 1], F32)
        w_parts = sb("w_parts", [P, 3, 2 * NBASE], BF16)
        small = sb("small", [P, 8, 64], F32)
        small_i = sb("small_i", [P, 64], I32)
        ge = sb("ge", [P, 256], BF16)
        dinv = sb("dinv", [P, 64], F32)
        stat = sb("stat", [P, 4, 64], F32)

        bank = [ctx.enter_context(nc.psum_tensor(f"bank{i}", [P, 512], F32)) for i in range(8)]
        SUMS = HALF
        tile_sum = lambda k: bank[k % SUMS][:, 0:D]
        w_ps = [bank[5], bank[6]]
        sorted_ps = bank[7]
        type_ps = bank[0][:, 0:P].bitcast(BF16)
        deg_ps = bank[7]
        turned = lambda k: bank[3 + k % 4][:, 0:D]
        before_ps, total_ps, blk_ps = bank[0], bank[1], bank[2]

        s_fill = sem("s_fill")
        s_iota = sem("s_iota")
        s_load = sem("s_load")
        s_x = sem("s_x")
        s_const = sem("s_const")
        s_hot = sem("s_hot")
        s_low = sem("s_low")
        s_lowused = sem("s_lowused")
        s_count = sem("s_count")
        s_cut = sem("s_cut")
        s_blk = sem("s_blk")
        s_group = sem("s_group")
        s_degmax = sem("s_degmax")
        s_root = sem("s_root")
        s_dinv = sem("s_dinv")
        s_y = sem("s_y")
        s_yt = sem("s_yt")
        s_ytc = sem("s_ytc")
        s_z = sem("s_z")
        s_zc = sem("s_zc")
        s_zw = [sem(f"s_zw{k}") for k in range(7)]
        s_zfree = sem("s_zfree")
        s_rec = sem("s_rec")
        s_put = sem("s_put")
        s_sorted = sem("s_sorted")
        s_decode = sem("s_decode")
        s_typet = sem("s_typet")
        s_typec = sem("s_typec")
        s_typeout = sem("s_typeout")
        s_typein = sem("s_typein")
        s_typehot = sem("s_typehot")
        s_wps = sem("s_wps")
        s_w = sem("s_w")
        s_actidle = sem("s_actidle")
        s_idx = sem("s_idx")
        s_gat = [sem(f"s_gat{k}") for k in range(TILE_U)]
        s_begun = sem("s_begun")
        s_row = sem("s_row")
        s_w0 = sem("s_w0")
        s_wb = sem("s_wb")
        s_sum = sem("s_sum")
        s_acc = sem("s_acc")
        s_fin = sem("s_fin")
        s_sq = sem("s_sq")
        s_var = sem("s_var")
        s_std = sem("s_std")
        s_outr = sem("s_outr")
        s_out = sem("s_out")

        block = ctx.enter_context(nc.Block())

        def bc(ap, shape):
            return ap.to_broadcast(shape)

        def inner(ap, n):
            return bc(ap.rearrange("p (a b) -> p a b", b=1), [ap.shape[0], ap.shape[1], n])

        def outer(ap, n):
            return bc(ap.rearrange("p (a b) -> p a b", a=1), [ap.shape[0], n, ap.shape[1]])

        @block.sync
        def _(sp):
            sp.wait_ge(s_fill, 6)
            whole, last = slice(0, (P - 1) * COLS), slice((P - 1) * COLS, E)
            for a, t in ((src, src_i), (dst, dst_i), (etype, typ_i)):
                sp.dma_start(t[0:P - 1, 0:COLS], a[whole].rearrange("(p c) -> p c", c=COLS)).then_inc(s_load, 16)
                sp.dma_start(t[P - 1:P, 0:LASTC], a[last].rearrange("(p c) -> p c", p=1)).then_inc(s_load, 16)
            for h in range(2):
                sp.dma_start(w_table[64 * h:64 * h + NREL, NBASE * h:NBASE * (h + 1)], comps).then_inc(s_load, 16)
                sp.dma_start(alpha_sb[64 * h:64 * h + NREL, :], alpha).then_inc(s_load, 16)
            sp.dma_start(bases_sb[:, :, :], bases.rearrange("b d f -> d b f")).then_inc(s_x, 16)
            full = (NB - 1) * P
            sp.dma_start(x_sb[:, 0:NB - 1, :], x[0:full, :].rearrange("(j p) d -> p j d", p=P)).then_inc(s_x, 16)
            sp.dma_start(x_sb[0:TAIL, NB - 1, :], x[full:N, :]).then_inc(s_x, 16)

            with sp.Fori(0, NB // 7) as i:
                for k in range(7):
                    sp.wait_ge(s_zc, i * 7 + (8 + k))
                    sp.dma_start(z_table[bass.ds(i * (7 * P) + k * P, P), :], z_ring[:, k, :]).then_inc(s_zw[k], 16)

            def spread_types(g):
                sp.wait_ge(s_typec, g + 1)
                sp.dma_start(type_rows.rearrange("h i s -> i h s"), type_t[0:PAIRS, :, :]).then_inc(s_typeout, 16)
                sp.wait_ge(s_typeout, g * 16 + 16)
                for h in range(2):
                    sp.dma_start(type_hot[64 * h:64 * h + 64, :],
                                 bc(type_rows[h:h + 1, :, :].rearrange("h i s -> h (i s)"), [64, PAIRS * P])
                                 ).then_inc(s_typein, 16)

            with sp.Fori(0, GROUPS) as g:
                spread_types(g)

            ch = 7
            for c in range(NB // ch):
                sp.wait_ge(s_outr, c + 1)
                j0 = c * ch
                if c < NB // ch - 1:
                    sp.dma_start(out[j0 * P:(j0 + ch) * P, :].rearrange("(j p) d -> p j d", p=P),
                                 x_sb[:, j0:j0 + ch, :]).then_inc(s_out, 16)
                else:
                    sp.dma_start(out[j0 * P:(j0 + ch - 1) * P, :].rearrange("(j p) d -> p j d", p=P),
                                 x_sb[:, j0:j0 + ch - 1, :]).then_inc(s_out, 16)
                    sp.dma_start(out[(j0 + ch - 1) * P:N, :], x_sb[0:TAIL, NB - 1, :]).then_inc(s_out, 16)
            sp.wait_ge(s_out, 16 * (NB // ch + 1))

        @block.gpsimd
        def _(pool):
            pool.memset(src_i[:, :], NB * P).then_inc(s_fill, 1)
            pool.memset(dst_i[:, :], 0).then_inc(s_fill, 1)
            pool.memset(typ_i[:, :], 0).then_inc(s_fill, 1)
            pool.memset(w_table[:, :], 0.0).then_inc(s_fill, 1)
            pool.memset(alpha_sb[:, :], 0.0).then_inc(s_fill, 1)
            pool.memset(x_sb[:, NB - 1, :], 0.0).then_inc(s_fill, 1)
            pool.iota(iota_i[:, :], [[1, 256]], base=0, channel_multiplier=0).then_inc(s_iota, 1)
            pool.iota(pcol_i[:, 0:1], [[1, 1]], base=0, channel_multiplier=1).then_inc(s_iota, 1)
            pool.memset(ones_b[:, :], 1.0).then_inc(s_iota, 1)
            pool.memset(zeros_b[:, :], 0.0).then_inc(s_iota, 1)
            pool.memset(records[:, :, :, :], 0.0).then_inc(s_iota, 1)
            pool.memset(idx_all[:, :], 0).then_inc(s_iota, 1)
            pool.memset(block_sum[:, :], 0.0).then_inc(s_iota, 1)
            for k in range(7):
                pool.wait_ge(s_zw[k], 16 * (NB // 7))
            with pool.Fori(0, GROUPS) as g:
                with pool.Fori(0, BODIES) as i:
                    for k in range(TILE_U):
                        if k % HALF == 0:
                            pool.wait_ge(s_idx, g * (2 * BODIES + 2) + i * 2 + (k // HALF + 1))
                        pool.wait_ge(s_sum, g * TILES + i * TILE_U + (k + 1))
                        pool.sem_inc(s_begun, 1)
                        pool.indirect_dma_start(
                            out=z_ring[:, k, :], out_offset=None, in_=z_table,
                            in_offset=bass.IndirectOffsetOnAxis(ap=idx_now[:, k:k + 1], axis=0),
                        ).then_inc(s_gat[k], 16)

        @block.scalar
        def _(act):
            act.sem_inc(s_ytc, 7)
            act.sem_inc(s_zc, 7)
            act.sem_inc(s_wb, TILE_U)
            act.sem_inc(s_actidle, 1)
            act.wait_ge(s_degmax, 1)
            act.activation(dinv[:, 0:NB], small[:, 6, 0:NB], ACT.Sqrt).then_inc(s_root, 1)
            act.wait_ge(s_dinv, 1)
            act.wait_ge(s_x, 48)
            with act.Fori(0, NB // 7) as i:
                def scale(k):
                    act.wait_ge(s_ytc, i * 7 + (k + 1))
                    act.activation(y_ring[:, k * D:(k + 1) * D], x_sb[:, bass.ds(i * 7 + k, 1), :].rearrange("p a d -> p (a d)"),
                                   ACT.Copy, scale=small[:, 7, bass.ds(i * 7 + k, 1)]).then_inc(s_y, 1)

                def copy_t(k):
                    act.wait_ge(s_yt, i * 7 + (k + 1))
                    act.wait_ge(s_zc, i * 7 + (k + 1))
                    act.activation(yt_ring[:, k * D:(k + 1) * D], turned(k),
                                   ACT.Copy).then_inc(s_ytc, 1)

                def copy_z(k):
                    act.wait_ge(s_z, i * 7 + (k + 1))
                    act.wait_ge(s_zw[k], i * 16)
                    act.activation(z_ring[:, k, :], bank[k % 3][:, :], ACT.Copy).then_inc(s_zc, 1)

                for k in range(9):
                    if k < 7:
                        scale(k)
                    if 1 <= k < 8:
                        copy_t(k - 1)
                    if k >= 2:
                        copy_z(k - 2)

            def weights(g):
                act.wait_ge(s_wps, g + 1)
                act.wait_ge(s_decode, g + 1)
                half = 64 * 2 * NBASE
                act.activation(w_all[:, 0:half], w_ps[0][:, 0:half], ACT.Copy).then_inc(s_w, 1)
                act.activation(w_all[:, half:], w_ps[1][:, 0:TILES * NBASE - half], ACT.Copy).then_inc(s_w, 1)
                act.wait_ge(s_w, g * 2 + 2)

            def stage_idx(h, at):
                act.activation(idx_now[:, h * HALF:(h + 1) * HALF], idx_all[:, bass.ds(at + h * HALF, HALF)],
                               ACT.Copy).then_inc(s_idx, 1)

            with act.Fori(0, GROUPS) as g:
                act.wait_ge(s_decode, g + 1)
                stage_idx(0, 0)
                stage_idx(1, 0)
                weights(g)
                with act.Fori(0, BODIES) as i:
                    act.drain()
                    act.activation(w_now[:, :], w_all[:, bass.ds(i * (TILE_U * NBASE), TILE_U * NBASE)], ACT.Copy)
                    act.drain()
                    for k in range(TILE_U):
                        act.wait_ge(s_row, g * TILES + i * TILE_U + (k + 1))
                        act.wait_ge(s_sum, g * TILES + i * TILE_U + (k + 1))
                        for b in range(1, NBASE):
                            o = (k * NBASE + b) * D
                            last = act.activation(wb[:, o:o + D], hot_row[:, k * D:(k + 1) * D], ACT.Copy,
                                                  scale=w_now[:, k * NBASE + b:k * NBASE + b + 1])
                        last.then_inc(s_wb, 1)
                        if k % HALF == HALF - 1:
                            act.wait_ge(s_gat[k], g * (16 * BODIES) + i * 16 + 16)
                            stage_idx(k // HALF, i * TILE_U + TILE_U)
                act.drain().then_inc(s_actidle, 1)

            act.wait_ge(s_fin, 1)
            act.activation(block_sum[:, 0:NB * D], x_sb[:, :, :].rearrange("p j d -> p (j d)"), ACT.Square).then_inc(s_sq, 1)
            act.wait_ge(s_var, 1)
            act.activation(stat[:, 1, 0:NB], stat[:, 0, 0:NB], ACT.Sqrt).then_inc(s_std, 1)

        @block.tensor
        def _(pe):
            pe.sem_inc(s_lowused, 2)
            pe.sem_inc(s_put, SRC_U)
            pe.sem_inc(s_sum, TILE_U)
            pe.wait_ge(s_const, 1)
            pe.matmul(deg_ps[:, 0:NB], zeros_b[:, 0:P], zeros_b[:, 0:NB], start=True, stop=False, skip_group_check=True)
            PART = SRC_G // 5
            with pe.Fori(0, GROUPS) as g:
                pe.wait_ge(s_hot, g * 5 + 5)
                for c in range(SRC_G // 10):
                    part = hot_blk[:, c * 10 * NB:(c + 1) * 10 * NB]
                    ends = dict(start=(c == 0), stop=(c == SRC_G // 10 - 1))
                    pe.matmul(before_ps[:, 0:10 * NB], below[:, :], part, **ends)
                    last = pe.matmul(total_ps[:, 0:10 * NB], ones_b[:, 0:P], part, **ends)
                last.then_inc(s_count, 1)
                for c in range(BODIES):
                    pe.wait_ge(s_low, g * BODIES + (c + 1))
                    for j in range(SRC_U):
                        col = c * SRC_U + j
                        at = ((c % 2) * SRC_U + j) * P
                        last = pe.matmul(deg_ps[:, 0:NB], hot_low[:, at:at + P], hot_blk[:, col * NB:(col + 1) * NB],
                                         start=False, stop=False, skip_group_check=True)
                    last.then_inc(s_lowused, 1)
                    if c == BODIES // 2:
                        pe.wait_ge(s_cut, g + 1)
                        pe.matmul(blk_ps[:, 0:TILES], ones_b[:, 0:P], ge[:, 0:TILES],
                                  start=True, stop=True).then_inc(s_blk, 1)
            pe.matmul(deg_ps[:, 0:NB], zeros_b[:, 0:P], zeros_b[:, 0:NB], start=False, stop=True,
                      skip_group_check=True).then_inc(s_count, 1)

            pe.wait_ge(s_x, 48)
            pe.wait_ge(s_group, GROUPS)
            with pe.Fori(0, NB // 7) as i:
                def turn(k):
                    pe.wait_ge(s_y, i * 7 + (k + 1))
                    pe.wait_ge(s_ytc, i * 7 + (k + 7))
                    pe.transpose(turned(k), y_ring[:, k * D:(k + 1) * D], ident_f[:, :]).then_inc(s_yt, 1)

                def times_bases(k):
                    pe.wait_ge(s_ytc, i * 7 + (k + 8))
                    pe.wait_ge(s_zc, i * 7 + (k + (7 if k == 0 else 5)))
                    pe.matmul(bank[k % 3][:, :], yt_ring[:, k * D:(k + 1) * D],
                              bases_sb[:, :, :].rearrange("p b f -> p (b f)"), start=True, stop=True).then_inc(s_z, 1)

                for k in range(8):
                    if k < 7:
                        turn(k)
                    if k >= 1:
                        times_bases(k - 1)

            def open_sort():
                pe.matmul(sorted_ps[:, 0:2 * TILES], zeros_b[:, 0:P], zeros_b[:, 0:2 * TILES],
                          start=True, stop=False, skip_group_check=True)

            def put(n8, k):
                pe.wait_ge(s_rec, n8 + (k + 1))
                pe.matmul(sorted_ps[:, 0:2 * TILES], hot_slot[:, k, :], hot_tile[:, k, :].bitcast(BF16),
                          start=False, stop=False, skip_group_check=True).then_inc(s_put, 1)

            def close_sort():
                pe.matmul(sorted_ps[:, 0:2 * TILES], zeros_b[:, 0:P], zeros_b[:, 0:2 * TILES],
                          start=False, stop=True, skip_group_check=True).then_inc(s_sorted, 1)

            def weights(g):
                pe.wait_ge(s_decode, g + 1)
                for h in range(2):
                    last = pe.transpose(type_ps[0:PAIRS, h * P:(h + 1) * P],
                                        type_b[:, h:TILES:2], ident_b[:, :])
                last.then_inc(s_typet, 1)
                pe.wait_ge(s_typehot, g + 1)
                for i in range(PAIRS):
                    o = (i % 64) * 2 * NBASE
                    for part in range(3):
                        last = pe.matmul(w_ps[i // 64][:, o:o + 2 * NBASE], type_hot[:, i * P:(i + 1) * P],
                                         w_parts[:, part, :], start=(part == 0), stop=(part == 2))
                last.then_inc(s_wps, 1)

            def tile(n10, k, n16):
                pe.wait_ge(s_w0, n10 + (k + 1))
                pe.wait_ge(s_wb, n10 + (k + 1 + TILE_U))
                pe.wait_ge(s_gat[k], n16 + 16)
                pe.wait_ge(s_acc, n10 + (k + 1 + TILE_U - SUMS))
                for b in range(NBASE):
                    o = (k * NBASE + b) * D
                    last = pe.matmul(tile_sum(k), wb[:, o:o + D], z_ring[:, k, b * D:(b + 1) * D],
                                     start=(b == 0), stop=(b == NBASE - 1))
                last.then_inc(s_sum, 1)

            pe.wait_ge(s_zc, NB + 7)
            open_sort()
            with pe.Fori(0, BODIES) as i:
                for k in range(SRC_U):
                    put(i * SRC_U, k)
            close_sort()
            with pe.Fori(0, GROUPS - 1) as g:
                weights(g)
                open_sort()
                with pe.Fori(0, BODIES) as i:
                    for k in range(TILE_U):
                        tile(g * TILES + i * TILE_U, k, g * (16 * BODIES) + i * 16)
                        for j in range(SRC_U):
                            if k == min(SRC_AT[j], TILE_U - 1):
                                put(g * SRC_G + i * SRC_U + SRC_G, j)
                close_sort()
            g = GROUPS - 1
            weights(g)
            with pe.Fori(0, BODIES) as i:
                for k in range(TILE_U):
                    tile(i * TILE_U + g * TILES, k, i * 16 + g * 16 * BODIES)

        @block.vector
        def _(dve):
            dve.sem_inc(s_acc, TILE_U)

            dve.wait_ge(s_iota, 7)
            dve.tensor_copy(iota_f[:, :], iota_i[:, :])
            dve.tensor_copy(pcol[:, 0:1], pcol_i[:, 0:1])
            dve.tensor_scalar(pcol_i[:, 1:2], pcol_i[:, 0:1], 63, None, ALU.bitwise_and)
            dve.drain()
            dve.tensor_copy(pcol[:, 1:2], pcol_i[:, 1:2])
            dve.tensor_copy(iota_b[:, :], iota_f[:, 0:P])
            dve.tensor_copy(iota_mark[:, :], iota_f[:, P:2 * P])
            dve.tensor_scalar(ident_f[:, :], iota_f[:, 0:P], pcol[:, 0:1], None, ALU.is_equal)
            dve.tensor_scalar(ident_b[:, :], iota_f[:, 0:P], pcol[:, 0:1], None, ALU.is_equal)
            dve.tensor_scalar(below[:, :], iota_f[:, 0:P], pcol[:, 0:1], None, ALU.is_gt)
            dve.memset(ge[:, :], 0.0)
            dve.drain().then_inc(s_const, 1)

            dve.wait_ge(s_load, 16 * 10)
            dve.tensor_scalar(w_table[:, :], w_table[:, :], alpha_sb[:, 0:1], None, ALU.mult)
            dve.drain()
            for part in range(3):
                dve.tensor_copy(w_parts[:, part, :], w_table[:, :])
                dve.drain()
                if part < 2:
                    dve.tensor_copy(w_rest[:, :], w_parts[:, part, :])
                    dve.drain()
                    dve.tensor_tensor(w_table[:, :], w_table[:, :], w_rest[:, :], ALU.subtract)
                    dve.drain()

            rec_i = records[:, :, 2, :].bitcast(I32)
            dve.tensor_scalar(typ_i[:, :], typ_i[:, :], 63, None, ALU.bitwise_and)
            dve.drain()
            low_i = z_ring[:, 0:2, :].rearrange("p a d -> p (a d)")[:, 0:ALLC].bitcast(I32)
            hi_i = z_ring[:, 2:4, :].rearrange("p a d -> p (a d)")[:, 0:ALLC].bitcast(I32)
            dve.tensor_scalar(low_i, src_i[:, :], P - 1, None, ALU.bitwise_and)
            dve.tensor_scalar(hi_i, src_i[:, :], 7, None, ALU.logical_shift_right)
            dve.drain()
            dve.tensor_copy(lo_b[:, :], low_i)
            dve.tensor_copy(hi_b[:, :], hi_i)
            dve.tensor_scalar(low_i, low_i, 6, None, ALU.logical_shift_left)
            dve.tensor_scalar(dst_i[:, :], dst_i[:, :], 16, (MARK << 16) | MARK, ALU.logical_shift_left, ALU.bitwise_or)
            dve.drain()
            dve.tensor_tensor(low_i, low_i, typ_i[:, :], ALU.bitwise_or)
            dve.drain()
            dve.tensor_tensor(dst_i[:, :], dst_i[:, :], low_i, ALU.bitwise_or)
            dve.drain()

            def put_records(parts, c0, c1):
                while c0 < c1:
                    b0, j0 = divmod(c0, SRC_U)
                    if j0 == 0 and c1 - c0 >= SRC_U:
                        nb = (c1 - c0) // SRC_U
                        dve.tensor_copy(rec_i[0:parts, b0:b0 + nb, :],
                                        dst_i[0:parts, c0:c0 + nb * SRC_U].rearrange("p (b j) -> p b j", j=SRC_U))
                        c0 += nb * SRC_U
                    else:
                        n = min(SRC_U - j0, c1 - c0)
                        dve.tensor_copy(rec_i[0:parts, b0, j0:j0 + n], dst_i[0:parts, c0:c0 + n])
                        c0 += n

            put_records(P, 0, LASTC)
            put_records(P - 1, LASTC, COLS)
            dve.drain()

            before, total, tiles_n, ends, base, endcol = (small[:, r, 0:NB] for r in range(6))
            with dve.Fori(0, GROUPS) as g:
                dve.wait_ge(s_lowused, g * BODIES + 2)
                dve.tensor_copy(hi_g[:, :], hi_b[:, bass.ds(g * SRC_G, SRC_G)])
                dve.tensor_copy(lo_g[:, :], lo_b[:, bass.ds(g * SRC_G, SRC_G)])
                dve.drain()
                q = SRC_G // 5
                for c in range(5):
                    dve.tensor_tensor(hot_blk[:, c * q * NB:(c + 1) * q * NB].rearrange("p (a b) -> p a b", b=NB),
                                      inner(hi_g[:, c * q:(c + 1) * q], NB), outer(iota_b[:, 0:NB], q),
                                      ALU.is_equal).then_inc(s_hot, 1)

                def low(c):
                    dve.wait_ge(s_lowused, g * BODIES + (c + 1))
                    at = (c % 2) * SRC_U * P
                    dve.tensor_tensor(hot_low[:, at:at + SRC_U * P].rearrange("p (a b) -> p a b", b=P),
                                      inner(lo_g[:, c * SRC_U:(c + 1) * SRC_U], P), outer(iota_b[:, :], SRC_U),
                                      ALU.is_equal).then_inc(s_low, 1)

                for c in range(3):
                    low(c)
                dve.wait_ge(s_count, g + 1)
                for ps, to in ((before_ps, before), (total_ps, total)):
                    dve.tensor_reduce(to, ps[:, 0:10 * NB].rearrange("p (r j) -> p j r", j=NB), AX.X, ALU.add)
                dve.drain()
                si = small_i[:, 0:NB]
                dve.tensor_scalar(si, total, float(P - 1), None, ALU.add)
                dve.drain()
                dve.tensor_scalar(si, si, 7, None, ALU.logical_shift_right)
                dve.drain()
                dve.tensor_copy(tiles_n, si)
                dve.drain()
                dve.tensor_tensor_scan(ends, ones_b[:, 0:NB], tiles_n, 0.0, ALU.mult, ALU.add)
                dve.drain()
                dve.tensor_tensor(base, ends, tiles_n, ALU.subtract)
                dve.tensor_tensor(small[0:NB, 7, 0:NB], ends[0:NB, :], ident_f[0:NB, 0:NB], ALU.mult)
                dve.drain()
                dve.tensor_scalar(base, base, float(P), -1.0, ALU.mult, ALU.add)
                dve.tensor_reduce(endcol[0:NB, 0:1], small[0:NB, 7, 0:NB], AX.X, ALU.add)
                dve.drain()
                dve.tensor_tensor(base, base, before, ALU.add)
                dve.tensor_scalar(ge[0:NB, 0:TILES], iota_f[0:NB, 0:TILES], endcol[0:NB, 0:1], None, ALU.is_ge).then_inc(s_cut, 1)
                dve.drain()
                for c in range(3, BODIES):
                    low(c)
                scan3 = slot_scan.rearrange("p (c j) -> p c j", j=NB)
                hot3 = hot_blk.rearrange("p (c j) -> p c j", j=NB)
                for j in range(NB):
                    dve.tensor_tensor_scan(scan3[:, :, j], ones_b[:, :], hot3[:, :, j], base[:, j:j + 1],
                                           ALU.mult, ALU.add)
                dve.drain()
                dve.tensor_tensor(slot_scan, slot_scan, hot_blk, ALU.mult)
                dve.drain()
                dve.tensor_reduce(slots := tmp_a[:, 0:SRC_G].bitcast(F32), scan3, AX.X, ALU.add)
                dve.drain()
                dve.tensor_copy(tmp_b[:, 0:SRC_G], slots)
                dve.drain()
                dve.tensor_scalar(tmp_a[:, 0:SRC_G], tmp_b[:, 0:SRC_G], 7, None, ALU.logical_shift_right)
                dve.tensor_scalar(tmp_b[:, 0:SRC_G], tmp_b[:, 0:SRC_G], P - 1, None, ALU.bitwise_and)
                dve.drain()
                for r, t in ((0, tmp_a), (1, tmp_b)):
                    dve.tensor_copy(records[:, bass.ds(g * BODIES, BODIES), r, :],
                                    t[:, 0:SRC_G].rearrange("p (b j) -> p b j", j=SRC_U))
                dve.wait_ge(s_blk, g + 1)
                dve.tensor_copy(blk_i[:, :], blk_ps[0:1, 0:TILES])
                dve.drain()
                b5 = blk_i[:, :].rearrange("p (w k) -> p w k", k=HALF)
                dve.tensor_copy(words_g[:, :], b5[:, :, HALF - 1])
                dve.drain()
                for k in range(HALF - 2, -1, -1):
                    dve.scalar_tensor_tensor(words_g[:, :], words_g[:, :], 6, b5[:, :, k],
                                             ALU.logical_shift_left, ALU.bitwise_or)
                    dve.drain()
                dve.tensor_copy(block_words[:, bass.ds(g * (2 * BODIES), 2 * BODIES)], words_g[:, :])
                dve.drain().then_inc(s_group, 1)

            dve.wait_ge(s_count, GROUPS + 1)
            dve.tensor_scalar(small[:, 6, 0:NB], deg_ps[:, 0:NB], 1.0, None, ALU.max).then_inc(s_degmax, 1)
            dve.tensor_scalar(small[:, 5, 0:NB], deg_ps[:, 0:NB], 0.0, None, ALU.is_gt)
            dve.wait_ge(s_root, 1)
            dve.reciprocal(small[:, 6, 0:NB], dinv[:, 0:NB])
            dve.drain()
            dve.tensor_tensor(small[:, 7, 0:NB], small[:, 6, 0:NB], small[:, 5, 0:NB], ALU.mult)
            dve.drain().then_inc(s_dinv, 1)

            def stage_src(body):
                dve.tensor_copy(src_now[:, :, :].rearrange("p r j -> p (r j)"), records[:, :, :, :].rearrange("p b r j -> p (b r j)")[:, bass.ds(body * (3 * SRC_U), 3 * SRC_U)])

            def hots_src(n8, k):
                dve.wait_ge(s_put, n8 + (k + 1))
                dve.tensor_scalar(hot_slot[:, k, :], iota_b[:, :], src_now[:, 1, k:k + 1], None, ALU.is_equal)
                dve.tensor_scalar(hot_tile[:, k, :], iota_f[:, 0:TILES], src_now[:, 0, k:k + 1],
                                  src_now[:, 2, k:k + 1], ALU.is_equal, ALU.mult).then_inc(s_rec, 1)

            def decode(g):
                dve.wait_ge(s_sorted, g + 1)
                dve.wait_ge(s_actidle, g + 1)
                halves = sorted_ps[:, 0:2 * TILES].bitcast(I32).rearrange("p (t h) -> p t h", h=2)
                dve.tensor_scalar(idx_all[:, 0:TILES], halves[:, :, 1], 16, LOW13, ALU.logical_shift_right, ALU.bitwise_and)
                dve.tensor_scalar(tmp_a[:, 0:TILES], halves[:, :, 0], 22, None, ALU.logical_shift_right)
                dve.tensor_scalar(tmp_b[:, 0:TILES], halves[:, :, 0], 16, 63, ALU.logical_shift_right, ALU.bitwise_and)
                dve.drain()
                dve.tensor_copy(row_all[:, :], tmp_a[:, 0:TILES])
                dve.tensor_copy(type_b[:, :], tmp_b[:, 0:TILES])
                dve.drain().then_inc(s_decode, 1)
                dve.wait_ge(s_typet, g + 1)
                dve.tensor_copy(type_t[0:PAIRS, :, :], type_ps[0:PAIRS, :].rearrange("p (h s) -> p h s", h=2)).then_inc(s_typec, 1)
                dve.wait_ge(s_typein, g * 32 + 32)
                dve.tensor_scalar(type_hot[:, :], type_hot[:, :], pcol[:, 1:2], None, ALU.is_equal).then_inc(s_typehot, 1)

            def hots_tile(n10, k):
                dve.wait_ge(s_wb, n10 + (k + 1))
                dve.tensor_scalar(hot_row[:, k * D:(k + 1) * D], iota_mark[:, :], row_now[:, k:k + 1], None,
                                  ALU.is_equal).then_inc(s_row, 1)
                dve.wait_ge(s_sum, n10 + (k + 1))
                o = k * NBASE * D
                dve.tensor_scalar(wb[:, o:o + D], iota_mark[:, :], row_now[:, k:k + 1], w0_now[:, k * NBASE:k * NBASE + 1],
                                  ALU.is_equal, ALU.mult).then_inc(s_w0, 1)

            def add_tile(n10, k, word):
                at = 6 * (k % HALF) - 7
                off = word & (63 << 6 * (k % HALF))
                off = (off >> at) if at >= 0 else (off << -at)
                off = dve.snap(off, min_val=0, max_val=NB * D)
                dst_ap = block_sum[:, bass.ds(off, D)]
                dve.wait_ge(s_sum, n10 + (k + 1 + TILE_U))
                dve.wait_ge(s_acc, n10 + (k + TILE_U))
                dve.tensor_tensor(dst_ap, tile_sum(k), dst_ap, ALU.add).then_inc(s_acc, 1)

            def main(g, with_sort):
                with dve.Fori(0, BODIES) as i:
                    n10 = i * TILE_U + g * TILES
                    n8 = i * SRC_U + (g + 1) * SRC_G
                    dve.drain()
                    if with_sort:
                        stage_src(i + (g + 1) * BODIES)
                    dve.tensor_copy(row_now[:, :], row_all[:, bass.ds(i * TILE_U, TILE_U)])
                    dve.wait_ge(s_w, g * 2 + 2)
                    dve.tensor_copy(w0_now[:, :], w_all[:, bass.ds(i * (TILE_U * NBASE), TILE_U * NBASE)])
                    words = [dve.value_load(block_words[0:1, bass.ds(i * 2 + g * (2 * BODIES) + h, 1)], min_val=0,
                                            max_val=(1 << 30) - 1) for h in range(2)]
                    dve.drain()
                    for k in range(TILE_U + LAG):
                        if k < TILE_U:
                            hots_tile(n10, k)
                        if with_sort and k in SRC_AT:
                            hots_src(n8, SRC_AT.index(k))
                        if k >= LAG:
                            add_tile(n10, k - LAG, words[(k - LAG) // HALF])

            with dve.Fori(0, BODIES) as i:
                dve.drain()
                stage_src(i)
                dve.drain()
                for k in range(SRC_U):
                    hots_src(i * SRC_U, k)
            with dve.Fori(0, GROUPS - 1) as g:
                decode(g)
                main(g, True)
            decode(GROUPS - 1)
            main(GROUPS - 1, False)
            dve.drain()

            sums = block_sum[:, 0:NB * D].rearrange("p (j d) -> p j d", d=D)
            dve.tensor_tensor(sums, sums, inner(small[:, 7, 0:NB], D), ALU.mult)
            dve.drain()
            dve.tensor_tensor(x_sb[:, :, :], x_sb[:, :, :], sums, ALU.add)
            dve.drain()
            dve.tensor_reduce(stat[:, 2, 0:NB], x_sb[:, :, :], AX.X, ALU.add)
            dve.drain()
            dve.tensor_scalar(stat[:, 2, 0:NB], stat[:, 2, 0:NB], 1.0 / D, None, ALU.mult)
            dve.drain()
            dve.tensor_tensor(x_sb[:, :, :], x_sb[:, :, :], inner(stat[:, 2, 0:NB], D), ALU.subtract)
            dve.drain().then_inc(s_fin, 1)
            dve.wait_ge(s_sq, 1)
            dve.tensor_reduce(stat[:, 0, 0:NB], sums, AX.X, ALU.add)
            dve.drain()
            dve.tensor_scalar(stat[:, 0, 0:NB], stat[:, 0, 0:NB], 1.0 / D, 1e-5, ALU.mult, ALU.add)
            dve.drain().then_inc(s_var, 1)
            dve.wait_ge(s_std, 1)
            dve.reciprocal(stat[:, 3, 0:NB], stat[:, 1, 0:NB])
            dve.drain()
            for c in range(NB // 7):
                j = slice(7 * c, 7 * c + 7)
                dve.tensor_tensor(x_sb[:, j, :], x_sb[:, j, :], inner(stat[:, 3, j], D), ALU.mult).then_inc(s_outr, 1)


def kernel(x, src, dst, edge_type_50, L0_gnn_bases, L0_gnn_comps, L0_gnn_alpha):
    import numpy as np
    import concourse.bacc as bacc
    from concourse.bass_utils import run_bass_kernel_spmd

    given = dict(x=x, src=src, dst=dst, etype=edge_type_50, bases=L0_gnn_bases, comps=L0_gnn_comps, alpha=L0_gnn_alpha)
    arrays = {name: np.ascontiguousarray(a) for name, a in given.items()}
    nc = bacc.Bacc("TRN2", target_bir_lowering=False, num_devices=1)
    aps = {name: nc.dram_tensor(name, a.shape, mybir.dt.from_np(a.dtype), kind="ExternalInput").ap()
           for name, a in arrays.items()}
    out = nc.dram_tensor("out", arrays["x"].shape, F32, kind="ExternalOutput").ap()
    relational_layer(nc, **aps, out=out)
    r = run_bass_kernel_spmd(nc, [arrays], core_ids=[0])
    return r.results[0]["out"]
```

```python
from contextlib import ExitStack

import concourse.bass as bass
from concourse import mybir

ALU = mybir.AluOpType
ACT = mybir.ActivationFunctionType
AX = mybir.AxisListType
F32 = mybir.dt.float32
BF16 = mybir.dt.bfloat16
I32 = mybir.dt.int32

P = 128
GROUPS = 4
BODIES = 25
SRC_U = 8
TILE_U = 10
HALF = TILE_U // 2
SRC_H = SRC_U // 2
SRC_AT = [0, 1, 3, 4, 5, 6, 8, 9]
STAGE_AT = (2, 7)
MARK = 0x2000
LOW13 = MARK - 1


def relational_layer(nc, x, src, dst, etype, bases, comps, alpha, out):
    N, D = x.shape
    E = src.shape[0]
    NBASE = bases.shape[0]
    NREL = comps.shape[0]
    ZW = NBASE * D
    NB = (N + P - 1) // P
    TAIL = N - (NB - 1) * P
    COLS = (E + P - 1) // P
    LASTC = E - (P - 1) * COLS
    SRC_G = BODIES * SRC_U
    TILES = BODIES * TILE_U
    ALLC = GROUPS * SRC_G
    PAIRS = TILES // 2
    ZB = 2 * BODIES
    assert D == P and N <= MARK and NREL <= 64 and NB <= min(63, ZB)
    assert ALLC >= COLS and 2 * TILES <= 512
    assert (SRC_G * P + NB * (P - 1)) // P <= TILES

    with ExitStack() as ctx:
        def sb(name, shape, dt):
            return ctx.enter_context(nc.sbuf_tensor(name, shape, dt))

        def sem(name):
            return ctx.enter_context(nc.semaphore(name))

        z_table = nc.dram_tensor("z_table", (ZB * P, ZW), F32).ap()
        type_rows = nc.dram_tensor("type_rows", (2, PAIRS, P), BF16).ap()

        x_sb = sb("x_sb", [P, ZB, D], F32)
        HOTS = NB * SRC_G // 2
        big = sb("big", [P, max(2 * HOTS, PAIRS * P // 2)], F32)
        hot_blk = big[:, 0:HOTS].bitcast(BF16)
        running = big[:, HOTS:2 * HOTS].bitcast(BF16)
        type_hot = big[:, 0:PAIRS * P // 2].bitcast(BF16)
        SUMW = 64 * D
        arena = sb("arena", [P, SUMW + TILE_U * (NBASE + 1) * D], F32)
        hot_low = arena[:, 0:P * SRC_G // 2].bitcast(BF16)
        block_sum = arena[:, 0:SUMW]
        work = arena[:, SUMW:]
        y_ring = work[:, 0:2 * D]
        yt_ring = work[:, 2 * D:4 * D]
        wb = work[:, 0:TILE_U * NBASE * D]
        hot_row = work[:, TILE_U * NBASE * D:]
        z_ring = sb("z_ring", [P, TILE_U, ZW], F32)
        src_i = sb("src_i", [P, ALLC], I32)
        dst_i = sb("dst_i", [P, ALLC], I32)
        typ_i = sb("typ_i", [P, ALLC], I32)
        hi_b = sb("hi_b", [P, ALLC], BF16)
        lo_b = sb("lo_b", [P, ALLC], BF16)
        hi_g = sb("hi_g", [P, SRC_G], BF16)
        lo_g = sb("lo_g", [P, SRC_G], BF16)
        records = sb("records", [P, ALLC // SRC_H + 2, 3, SRC_H], F32)
        idx_all = sb("idx_all", [P, TILES + TILE_U], I32)
        lists = sb("lists", [P, 2 * BODIES + 2, HALF * (1 + NBASE)], F32)
        tmp_a = sb("tmp_a", [P, 256], I32)
        tmp_b = sb("tmp_b", [P, 256], I32)
        type_b = sb("type_b", [P, TILES], BF16)
        type_t = sb("type_t", [P, 2, P], BF16)
        block_words = sb("block_words", [1, 2 + GROUPS * 2 * BODIES], I32)
        words_g = sb("words_g", [1, 2 * BODIES], I32)
        blk_i = sb("blk_i", [1, TILES], I32)
        hot_slot = sb("hot_slot", [P, SRC_U, P], BF16)
        hot_tile = sb("hot_tile", [P, SRC_U, TILES], F32)
        first_of = hot_tile[:, :, 0:SRC_G]
        src_now = sb("src_now", [P, 2, 3, SRC_H], F32)
        list_now = sb("list_now", [P, 2, HALF * (1 + NBASE)], F32)
        idx_now = sb("idx_now", [P, TILE_U], I32)
        bases_sb = sb("bases_sb", [P, NBASE, D], F32)
        iota_i = sb("iota_i", [P, 256], I32)
        pcol_i = sb("pcol_i", [P, 2], I32)
        pcol = sb("pcol", [P, 2], F32)
        iota_f = sb("iota_f", [P, 256], F32)
        iota_b = sb("iota_b", [P, P], BF16)
        iota_mark = sb("iota_mark", [P, P], BF16)
        ident_f = sb("ident_f", [P, P], F32)
        ident_b = sb("ident_b", [P, P], BF16)
        below = sb("below", [P, P], BF16)
        ones_b = sb("ones_b", [P, SRC_G], BF16)
        zeros_b = sb("zeros_b", [P, 512], BF16)
        w_table = sb("w_table", [P, 2 * NBASE], F32)
        w_rest = sb("w_rest", [P, 2 * NBASE], F32)
        alpha_sb = sb("alpha_sb", [P, 1], F32)
        w_parts = sb("w_parts", [P, 3, 2 * NBASE], BF16)
        small = sb("small", [P, 8, 64], F32)
        small_i = sb("small_i", [P, 64], I32)
        ge = sb("ge", [P, 256], BF16)
        dinv = sb("dinv", [P, 64], F32)
        stat = sb("stat", [P, 4, 64], F32)

        bank = [ctx.enter_context(nc.psum_tensor(f"bank{i}", [P, 512], F32)) for i in range(8)]
        SUMS = HALF
        tile_sum = lambda k: bank[k % SUMS][:, 0:D]
        w_ps = [bank[5], bank[6]]
        sorted_ps = bank[7]
        type_ps = bank[5][:, 0:P].bitcast(BF16)
        deg_ps = bank[7]
        turned = lambda k: bank[3 + k][:, 0:D]
        before_ps, total_ps, blk_ps, slot_ps = bank[0], bank[1], bank[2], bank[3]

        s_fill = sem("s_fill")
        s_iota = sem("s_iota")
        s_load = sem("s_load")
        s_x = sem("s_x")
        s_const = sem("s_const")
        s_hot = sem("s_hot")
        s_low = sem("s_low")
        s_deg = sem("s_deg")
        s_base = sem("s_base")
        s_first = sem("s_first")
        s_firstused = sem("s_firstused")
        s_rank = sem("s_rank")
        s_slot = sem("s_slot")
        s_clear = sem("s_clear")
        s_count = sem("s_count")
        s_cut = sem("s_cut")
        s_blk = sem("s_blk")
        s_group = sem("s_group")
        s_degmax = sem("s_degmax")
        s_root = sem("s_root")
        s_dinv = sem("s_dinv")
        s_y = sem("s_y")
        s_yt = sem("s_yt")
        s_ytc = sem("s_ytc")
        s_z = sem("s_z")
        s_zc = sem("s_zc")
        s_zw = [sem(f"s_zw{k}") for k in range(2)]
        s_rec = sem("s_rec")
        s_put = sem("s_put")
        s_sorted = sem("s_sorted")
        s_decode = sem("s_decode")
        s_typet = sem("s_typet")
        s_typec = sem("s_typec")
        s_typeout = sem("s_typeout")
        s_typein = sem("s_typein")
        s_typehot = sem("s_typehot")
        s_wps = sem("s_wps")
        s_w = sem("s_w")
        s_actidle = sem("s_actidle")
        s_idx = sem("s_idx")
        s_gat = [sem(f"s_gat{k}") for k in range(TILE_U)]
        s_begun = sem("s_begun")
        s_row = sem("s_row")
        s_wb = sem("s_wb")
        s_list = sem("s_list")
        s_src = sem("s_src")
        s_sum = sem("s_sum")
        s_acc = sem("s_acc")
        s_fin = sem("s_fin")
        s_sq = sem("s_sq")
        s_var = sem("s_var")
        s_std = sem("s_std")
        s_outr = sem("s_outr")
        s_out = sem("s_out")

        block = ctx.enter_context(nc.Block())

        def bc(ap, shape):
            return ap.to_broadcast(shape)

        def inner(ap, n):
            return bc(ap.rearrange("p (a b) -> p a b", b=1), [ap.shape[0], ap.shape[1], n])

        def outer(ap, n):
            return bc(ap.rearrange("p (a b) -> p a b", a=1), [ap.shape[0], n, ap.shape[1]])

        @block.sync
        def _(sp):
            sp.wait_ge(s_fill, 6)
            whole, last = slice(0, (P - 1) * COLS), slice((P - 1) * COLS, E)
            for a, t in ((src, src_i), (dst, dst_i), (etype, typ_i)):
                sp.dma_start(t[0:P - 1, 0:COLS], a[whole].rearrange("(p c) -> p c", c=COLS)).then_inc(s_load, 16)
                sp.dma_start(t[P - 1:P, 0:LASTC], a[last].rearrange("(p c) -> p c", p=1)).then_inc(s_load, 16)
            for h in range(2):
                sp.dma_start(w_table[64 * h:64 * h + NREL, NBASE * h:NBASE * (h + 1)], comps).then_inc(s_load, 16)
                sp.dma_start(alpha_sb[64 * h:64 * h + NREL, :], alpha).then_inc(s_load, 16)
            full = (NB - 1) * P
            sp.dma_start(x_sb[:, 0:NB - 1, :], x[0:full, :].rearrange("(j p) d -> p j d", p=P)).then_inc(s_x, 16)
            sp.dma_start(x_sb[0:TAIL, NB - 1, :], x[full:N, :]).then_inc(s_x, 16)

            with sp.Fori(0, BODIES) as i:
                for k in range(2):
                    sp.wait_ge(s_zc, i * 2 + (k + 3))
                    sp.dma_start(z_table[bass.ds(i * (2 * P) + k * P, P), :], z_ring[:, k, :]).then_inc(s_zw[k], 16)

            def spread_types(g):
                sp.wait_ge(s_typec, g + 1)
                sp.dma_start(type_rows.rearrange("h i s -> i h s"), type_t[0:PAIRS, :, :]).then_inc(s_typeout, 16)
                sp.wait_ge(s_typeout, g * 16 + 16)
                for h in range(2):
                    sp.dma_start(type_hot[64 * h:64 * h + 64, :],
                                 bc(type_rows[h:h + 1, :, :].rearrange("h i s -> h (i s)"), [64, PAIRS * P])
                                 ).then_inc(s_typein, 16)

            with sp.Fori(0, GROUPS) as g:
                spread_types(g)

            ch = 7
            for c in range(NB // ch):
                sp.wait_ge(s_outr, c + 1)
                j0 = c * ch
                if c < NB // ch - 1:
                    sp.dma_start(out[j0 * P:(j0 + ch) * P, :].rearrange("(j p) d -> p j d", p=P),
                                 x_sb[:, j0:j0 + ch, :]).then_inc(s_out, 16)
                else:
                    sp.dma_start(out[j0 * P:(j0 + ch - 1) * P, :].rearrange("(j p) d -> p j d", p=P),
                                 x_sb[:, j0:j0 + ch - 1, :]).then_inc(s_out, 16)
                    sp.dma_start(out[(j0 + ch - 1) * P:N, :], x_sb[0:TAIL, NB - 1, :]).then_inc(s_out, 16)
            sp.wait_ge(s_out, 16 * (NB // ch + 1))

        @block.gpsimd
        def _(pool):
            pool.dma_start(bases_sb[:, :, :], bases.rearrange("b d f -> d b f")).then_inc(s_gat[TILE_U - 1], 16)
            pool.memset(src_i[:, :], NB * P).then_inc(s_fill, 1)
            pool.memset(dst_i[:, :], 0).then_inc(s_fill, 1)
            pool.memset(typ_i[:, :], 0).then_inc(s_fill, 1)
            pool.memset(w_table[:, :], 0.0).then_inc(s_fill, 1)
            pool.memset(alpha_sb[:, :], 0.0).then_inc(s_fill, 1)
            pool.memset(x_sb[:, NB - 1:ZB, :].rearrange("p j d -> p (j d)"), 0.0).then_inc(s_fill, 1)
            pool.iota(iota_i[:, :], [[1, 256]], base=0, channel_multiplier=0).then_inc(s_iota, 1)
            pool.iota(pcol_i[:, 0:1], [[1, 1]], base=0, channel_multiplier=1).then_inc(s_iota, 1)
            pool.memset(ones_b[:, :], 1.0).then_inc(s_iota, 1)
            pool.memset(zeros_b[:, :], 0.0).then_inc(s_iota, 1)
            pool.memset(lists[:, :, :], 0.0).then_inc(s_iota, 1)
            pool.memset(records[:, :, :, :], 0.0).then_inc(s_iota, 1)
            pool.memset(idx_all[:, :], 0).then_inc(s_iota, 1)
            pool.wait_ge(s_deg, GROUPS + 1)
            pool.memset(block_sum, 0.0).then_inc(s_clear, 1)
            for k in range(2):
                pool.wait_ge(s_zw[k], 16 * BODIES + 16)
            with pool.Fori(0, GROUPS) as g:
                with pool.Fori(0, BODIES) as i:
                    for k in range(TILE_U):
                        if k % HALF == 0:
                            pool.wait_ge(s_idx, g * (2 * BODIES + 1) + i * 2 + (k // HALF + 1))
                        pool.wait_ge(s_sum, g * TILES + i * TILE_U + (k + 1))
                        pool.sem_inc(s_begun, 1)
                        pool.indirect_dma_start(
                            out=z_ring[:, k, :], out_offset=None, in_=z_table,
                            in_offset=bass.IndirectOffsetOnAxis(ap=idx_now[:, k:k + 1], axis=0),
                        ).then_inc(s_gat[k], 16)

        @block.scalar
        def _(act):
            act.sem_inc(s_ytc, 2)
            act.sem_inc(s_zc, 2)
            for k in range(2):
                act.sem_inc(s_zw[k], 16)
            act.sem_inc(s_wb, TILE_U)
            act.sem_inc(s_actidle, 1)
            with act.Fori(0, GROUPS) as g:
                act.wait_ge(s_base, g + 1)
                for j in range(NB):
                    act.wait_ge(s_firstused, g * NB + (j + 1))
                    act.activation(first_of[:, j % SRC_U, :], hot_blk[:, j * SRC_G:(j + 1) * SRC_G], ACT.Copy,
                                   scale=small[:, 4, j:j + 1]).then_inc(s_first, 1)
            act.wait_ge(s_degmax, 1)
            act.activation(dinv[:, 0:NB], small[:, 6, 0:NB], ACT.Sqrt).then_inc(s_root, 1)
            act.wait_ge(s_dinv, 1)
            act.wait_ge(s_x, 32)
            with act.Fori(0, BODIES) as i:
                for k in range(2):
                    act.activation(y_ring[:, k * D:(k + 1) * D], x_sb[:, :, :].rearrange("p j d -> p (j d)")[:, bass.ds(i * (2 * D) + k * D, D)],
                                   ACT.Copy, scale=small[:, 7, bass.ds(i * 2 + k, 1)]).then_inc(s_y, 1)
                for k in range(2):
                    act.wait_ge(s_yt, i * 2 + (k + 1))
                    act.activation(yt_ring[:, k * D:(k + 1) * D], turned(k), ACT.Copy).then_inc(s_ytc, 1)
                for k in range(2):
                    act.wait_ge(s_z, i * 2 + (k + 1))
                    act.wait_ge(s_zw[k], i * 16 + 16)
                    act.activation(z_ring[:, k, :], bank[k][:, :], ACT.Copy).then_inc(s_zc, 1)

            def weights(g):
                act.wait_ge(s_wps, g + 1)
                full, cut = divmod(128, HALF)
                w_of = lambda h0, h1, t0, t1: lists[:, h0:h1, HALF + t0 * NBASE:HALF + t1 * NBASE]
                nb = NBASE
                last = 2 * BODIES
                for to, frm in (
                    (w_of(0, full, 0, HALF), w_ps[0][:, 0:full * HALF * nb].rearrange("p (h w) -> p h w", h=full)),
                    (w_of(full, full + 1, 0, cut), w_ps[0][:, full * HALF * nb:128 * nb].rearrange("p (h w) -> p h w", h=1)),
                    (w_of(full, full + 1, cut, HALF), w_ps[1][:, 0:(HALF - cut) * nb].rearrange("p (h w) -> p h w", h=1)),
                    (w_of(full + 1, last, 0, HALF), w_ps[1][:, (HALF - cut) * nb:(TILES - 128) * nb].rearrange(
                        "p (h w) -> p h w", h=last - full - 1)),
                ):
                    ins = act.activation(to, frm, ACT.Copy)
                ins.then_inc(s_w, 1)

            def stage_idx(h, at):
                act.activation(idx_now[:, h * HALF:(h + 1) * HALF], idx_all[:, bass.ds(at, HALF)],
                               ACT.Copy).then_inc(s_idx, 1)

            with act.Fori(0, GROUPS) as g:
                act.wait_ge(s_decode, g + 1)
                stage_idx(0, 0)
                weights(g)
                with act.Fori(0, BODIES) as i:
                    n10 = act.snap(g * TILES + i * TILE_U)
                    for k in range(TILE_U):
                        act.wait_ge(s_row, n10 + (k + 1))
                        for b in range(1, NBASE):
                            o = (k * NBASE + b) * D
                            at = HALF + (k % HALF) * NBASE + b
                            last = act.activation(wb[:, o:o + D], hot_row[:, k * D:(k + 1) * D], ACT.Copy,
                                                  scale=list_now[:, k // HALF, at:at + 1])
                        last.then_inc(s_wb, 1)
                        if k == STAGE_AT[0]:
                            act.wait_ge(s_gat[TILE_U - 1], g * (16 * BODIES) + i * 16 + 16)
                            stage_idx(1, i * TILE_U + HALF)
                        if k == STAGE_AT[1]:
                            act.wait_ge(s_gat[HALF - 1], g * (16 * BODIES) + i * 16 + 16)
                            stage_idx(0, i * TILE_U + TILE_U)
                act.drain().then_inc(s_actidle, 1)

            act.wait_ge(s_fin, 1)
            act.activation(block_sum[:, 0:NB * D], x_sb[:, 0:NB, :].rearrange("p j d -> p (j d)"), ACT.Square).then_inc(s_sq, 1)
            act.wait_ge(s_var, 1)
            act.activation(stat[:, 1, 0:NB], stat[:, 0, 0:NB], ACT.Sqrt).then_inc(s_std, 1)

        @block.tensor
        def _(pe):
            pe.sem_inc(s_deg, 1)
            pe.sem_inc(s_firstused, SRC_U)
            pe.sem_inc(s_put, SRC_U)
            pe.sem_inc(s_sum, TILE_U)
            pe.wait_ge(s_const, 1)
            pe.matmul(deg_ps[:, 0:NB], zeros_b[:, 0:P], zeros_b[:, 0:NB], start=True, stop=False, skip_group_check=True)
            hot_jc = hot_blk.rearrange("p (j c) -> p j c", c=SRC_G)
            low_rc = hot_low.rearrange("p (r c) -> p r c", c=SRC_G)
            with pe.Fori(0, GROUPS) as g:
                pe.wait_ge(s_hot, g + 1)
                for c in range(0, SRC_G, 10):
                    part = hot_jc[:, :, c:c + 10]
                    ends = dict(start=(c == 0), stop=(c == SRC_G - 10))
                    pe.matmul(before_ps[:, 0:10 * NB].rearrange("p (j r) -> p j r", r=10), below[:, :], part, **ends)
                    last = pe.matmul(total_ps[:, 0:10 * NB].rearrange("p (j r) -> p j r", r=10), ones_b[:, 0:P], part, **ends)
                last.then_inc(s_count, 1)
                pe.wait_ge(s_cut, g + 1)
                pe.matmul(blk_ps[:, 0:TILES], ones_b[:, 0:P], ge[:, 0:TILES], start=True, stop=True).then_inc(s_blk, 1)
                for j in range(NB):
                    pe.wait_ge(s_first, g * NB + (j + 1))
                    pe.matmul(slot_ps[:, 0:SRC_G], ident_f[:, :], first_of[:, j % SRC_U, :],
                              start=(j == 0), stop=False).then_inc(s_firstused, 1)
                pe.wait_ge(s_rank, g + 1)
                for j in range(NB):
                    last = pe.matmul(slot_ps[:, 0:SRC_G], ident_b[:, :], running[:, j * SRC_G:(j + 1) * SRC_G],
                                     start=False, stop=(j == NB - 1))
                last.then_inc(s_slot, 1)
                pe.wait_ge(s_low, g + 1)
                for c in range(SRC_G):
                    last = pe.matmul(deg_ps[:, 0:NB], low_rc[:, :, c], hot_jc[:, :, c],
                                     start=False, stop=False, skip_group_check=True)
                last.then_inc(s_deg, 1)
            pe.matmul(deg_ps[:, 0:NB], zeros_b[:, 0:P], zeros_b[:, 0:NB], start=False, stop=True,
                      skip_group_check=True).then_inc(s_count, 1)

            def open_sort():
                pe.matmul(sorted_ps[:, 0:2 * TILES], zeros_b[:, 0:P], zeros_b[:, 0:2 * TILES],
                          start=True, stop=False, skip_group_check=True)

            def put(n8, k):
                pe.wait_ge(s_rec, n8 + (k + 2))
                pe.matmul(sorted_ps[:, 0:2 * TILES], hot_slot[:, k, :], hot_tile[:, k, :].bitcast(BF16),
                          start=False, stop=False, skip_group_check=True).then_inc(s_put, 1)

            def close_sort():
                pe.matmul(sorted_ps[:, 0:2 * TILES], zeros_b[:, 0:P], zeros_b[:, 0:2 * TILES],
                          start=False, stop=True, skip_group_check=True).then_inc(s_sorted, 1)

            def weights(g):
                pe.wait_ge(s_decode, g + 1)
                for h in range(2):
                    last = pe.transpose(type_ps[0:PAIRS, h * P:(h + 1) * P],
                                        type_b[:, h:TILES:2], ident_b[:, :])
                last.then_inc(s_typet, 1)
                pe.wait_ge(s_typehot, g + 1)
                for i in range(PAIRS):
                    o = (i % 64) * 2 * NBASE
                    for part in range(3):
                        last = pe.matmul(w_ps[i // 64][:, o:o + 2 * NBASE], type_hot[:, i * P:(i + 1) * P],
                                         w_parts[:, part, :], start=(part == 0), stop=(part == 2))
                last.then_inc(s_wps, 1)

            def tile(n10, k, n16):
                pe.wait_ge(s_wb, n10 + (k + 1 + TILE_U))
                pe.wait_ge(s_gat[k], n16 + (32 if k == TILE_U - 1 else 16))
                for b in range(NBASE):
                    o = (k * NBASE + b) * D
                    last = pe.matmul(tile_sum(k), wb[:, o:o + D], z_ring[:, k, b * D:(b + 1) * D],
                                     start=(b == 0), stop=(b == NBASE - 1))
                last.then_inc(s_sum, 1)

            pe.wait_ge(s_gat[TILE_U - 1], 16)
            pe.wait_ge(s_group, GROUPS)
            pe.matmul(bank[2][:, 0:D], zeros_b[:, 0:P], zeros_b[:, 0:D], start=True, stop=True)
            pe.wait_ge(s_dinv, 1)
            open_sort()
            with pe.Fori(0, BODIES) as i:
                for k in range(2):
                    pe.wait_ge(s_y, i * 2 + (k + 1))
                    pe.wait_ge(s_ytc, i * 2 + (k + 1))
                    pe.transpose(turned(k), y_ring[:, k * D:(k + 1) * D], ident_f[:, :]).then_inc(s_yt, 1)
                    put(i * SRC_U, 4 * k)
                    put(i * SRC_U, 4 * k + 1)
                    pe.wait_ge(s_ytc, i * 2 + (k + 3))
                    pe.wait_ge(s_zc, i * 2 + (k + 1))
                    pe.matmul(bank[k][:, :], yt_ring[:, k * D:(k + 1) * D],
                              bases_sb[:, :, :].rearrange("p b f -> p (b f)"), start=True, stop=True).then_inc(s_z, 1)
                    put(i * SRC_U, 4 * k + 2)
                    put(i * SRC_U, 4 * k + 3)
            close_sort()
            pe.wait_ge(s_zc, 2 * BODIES + 2)
            with pe.Fori(0, GROUPS - 1) as g:
                weights(g)
                open_sort()
                with pe.Fori(0, BODIES) as i:
                    for k in range(TILE_U):
                        tile(g * TILES + i * TILE_U, k, g * (16 * BODIES) + i * 16)
                        if k in SRC_AT:
                            put(g * SRC_G + i * SRC_U + SRC_G, SRC_AT.index(k))
                close_sort()
            g = GROUPS - 1
            weights(g)
            with pe.Fori(0, BODIES) as i:
                for k in range(TILE_U):
                    tile(i * TILE_U + g * TILES, k, i * 16 + g * 16 * BODIES)

        @block.vector
        def _(dve):
            dve.sem_inc(s_acc, 1)
            dve.sem_inc(s_rec, 1)

            dve.wait_ge(s_iota, 7)
            dve.tensor_copy(iota_f[:, :], iota_i[:, :])
            dve.tensor_copy(pcol[:, 0:1], pcol_i[:, 0:1])
            dve.tensor_scalar(pcol_i[:, 1:2], pcol_i[:, 0:1], 63, None, ALU.bitwise_and)
            dve.drain()
            dve.tensor_copy(pcol[:, 1:2], pcol_i[:, 1:2])
            dve.tensor_copy(iota_b[:, :], iota_f[:, 0:P])
            dve.tensor_copy(iota_mark[:, :], iota_f[:, P:2 * P])
            dve.tensor_scalar(ident_f[:, :], iota_f[:, 0:P], pcol[:, 0:1], None, ALU.is_equal)
            dve.tensor_scalar(ident_b[:, :], iota_f[:, 0:P], pcol[:, 0:1], None, ALU.is_equal)
            dve.tensor_scalar(below[:, :], iota_f[:, 0:P], pcol[:, 0:1], None, ALU.is_gt)
            dve.memset(ge[:, :], 0.0)
            dve.drain().then_inc(s_const, 1)

            dve.wait_ge(s_load, 16 * 10)
            dve.tensor_scalar(w_table[:, :], w_table[:, :], alpha_sb[:, 0:1], None, ALU.mult)
            dve.drain()
            for part in range(3):
                dve.tensor_copy(w_parts[:, part, :], w_table[:, :])
                dve.drain()
                if part < 2:
                    dve.tensor_copy(w_rest[:, :], w_parts[:, part, :])
                    dve.drain()
                    dve.tensor_tensor(w_table[:, :], w_table[:, :], w_rest[:, :], ALU.subtract)
                    dve.drain()

            dve.tensor_scalar(typ_i[:, :], typ_i[:, :], 63, None, ALU.bitwise_and)
            dve.drain()
            low_i = z_ring[:, 0:2, :].rearrange("p a d -> p (a d)")[:, 0:ALLC].bitcast(I32)
            hi_i = z_ring[:, 2:4, :].rearrange("p a d -> p (a d)")[:, 0:ALLC].bitcast(I32)
            dve.tensor_scalar(low_i, src_i[:, :], P - 1, None, ALU.bitwise_and)
            dve.tensor_scalar(hi_i, src_i[:, :], 7, None, ALU.logical_shift_right)
            dve.drain()
            dve.tensor_copy(lo_b[:, :], low_i)
            dve.tensor_copy(hi_b[:, :], hi_i)
            dve.tensor_scalar(low_i, low_i, 6, None, ALU.logical_shift_left)
            dve.tensor_scalar(dst_i[:, :], dst_i[:, :], 16, (MARK << 16) | MARK, ALU.logical_shift_left, ALU.bitwise_or)
            dve.drain()
            dve.tensor_tensor(low_i, low_i, typ_i[:, :], ALU.bitwise_or)
            dve.drain()
            dve.tensor_tensor(dst_i[:, :], dst_i[:, :], low_i, ALU.bitwise_or)
            dve.drain()

            rec_i = records[:, :, 2, :].bitcast(I32)

            def put_records(parts, c0, c1):
                while c0 < c1:
                    b0, j0 = divmod(c0, SRC_H)
                    whole = (c1 - c0) // SRC_H * SRC_H if j0 == 0 else 0
                    n = whole or min(SRC_H - j0, c1 - c0)
                    dve.tensor_copy(rec_i[0:parts, b0:b0 + max(1, n // SRC_H), j0:j0 + min(n, SRC_H)],
                                    dst_i[0:parts, c0:c0 + n].rearrange("p (b j) -> p b j", j=min(n, SRC_H)))
                    c0 += n

            put_records(P, 0, LASTC)
            put_records(P - 1, LASTC, COLS)
            dve.drain()

            dve.memset(block_words[:, 0:2], NB)
            dve.drain()
            for _ in range(HALF - 1):
                dve.tensor_scalar(block_words[:, 0:2], block_words[:, 0:2], 6, NB, ALU.logical_shift_left, ALU.bitwise_or)
                dve.drain()
            dve.memset(small[:, 7, :], 0.0)

            before, total, tiles_n, ends, base, endcol = (small[:, r, 0:NB] for r in range(6))
            with dve.Fori(0, GROUPS) as g:
                dve.wait_ge(s_deg, g + 1)
                dve.tensor_copy(hi_g[:, :], hi_b[:, bass.ds(g * SRC_G, SRC_G)])
                dve.tensor_copy(lo_g[:, :], lo_b[:, bass.ds(g * SRC_G, SRC_G)])
                dve.drain()
                for j in range(NB):
                    dve.tensor_scalar(hot_blk[:, j * SRC_G:(j + 1) * SRC_G], hi_g[:, :], float(j), None, ALU.is_equal)
                dve.drain().then_inc(s_hot, 1)
                dve.tensor_tensor_scan(running, ones_b[:, 0:1].to_broadcast([P, NB * SRC_G]), hot_blk, 0.0, ALU.mult, ALU.add)
                dve.wait_ge(s_count, g + 1)
                for ps, to in ((before_ps, before), (total_ps, total)):
                    dve.tensor_reduce(to, ps[:, 0:10 * NB].rearrange("p (j r) -> p j r", r=10), AX.X, ALU.add)
                dve.drain()
                si = small_i[:, 0:NB]
                dve.tensor_scalar(si, total, float(P - 1), None, ALU.add)
                dve.drain()
                dve.tensor_scalar(si, si, 7, None, ALU.logical_shift_right)
                dve.drain()
                dve.tensor_copy(tiles_n, si)
                dve.drain()
                dve.tensor_tensor_scan(ends, ones_b[:, 0:NB], tiles_n, 0.0, ALU.mult, ALU.add)
                dve.drain()
                dve.tensor_tensor(base, ends, tiles_n, ALU.subtract)
                dve.tensor_tensor(small[0:NB, 6, 0:NB], ends[0:NB, :], ident_f[0:NB, 0:NB], ALU.mult)
                dve.drain()
                dve.tensor_scalar(base, base, float(P), -1.0, ALU.mult, ALU.add)
                dve.tensor_reduce(endcol[0:NB, 0:1], small[0:NB, 6, 0:NB], AX.X, ALU.add)
                dve.drain()
                dve.tensor_tensor(base, base, before, ALU.add)
                dve.drain()
                dve.tensor_tensor(base[:, 1:NB], base[:, 1:NB], running[:, SRC_G - 1:(NB - 1) * SRC_G:SRC_G], ALU.subtract)
                dve.drain().then_inc(s_base, 1)
                dve.tensor_scalar(ge[0:NB, 0:TILES], iota_f[0:NB, 0:TILES], endcol[0:NB, 0:1], None, ALU.is_ge).then_inc(s_cut, 1)
                dve.drain()
                dve.tensor_tensor(running, running, hot_blk, ALU.mult).then_inc(s_rank, 1)
                for row in range(P):
                    dve.tensor_scalar(hot_low[:, row * SRC_G:(row + 1) * SRC_G], lo_g[:, :], float(row), None, ALU.is_equal)
                dve.drain().then_inc(s_low, 1)
                dve.wait_ge(s_slot, g + 1)
                dve.tensor_copy(tmp_b[:, 0:SRC_G], slot_ps[:, 0:SRC_G])
                dve.drain()
                dve.tensor_scalar(tmp_a[:, 0:SRC_G], tmp_b[:, 0:SRC_G], 7, None, ALU.logical_shift_right)
                dve.tensor_scalar(tmp_b[:, 0:SRC_G], tmp_b[:, 0:SRC_G], P - 1, None, ALU.bitwise_and)
                dve.drain()
                for r, t in ((0, tmp_a), (1, tmp_b)):
                    dve.tensor_copy(records[:, bass.ds(g * (2 * BODIES), 2 * BODIES), r, :],
                                    t[:, 0:SRC_G].rearrange("p (b j) -> p b j", j=SRC_H))
                dve.wait_ge(s_blk, g + 1)
                dve.tensor_copy(blk_i[:, :], blk_ps[0:1, 0:TILES])
                dve.drain()
                b5 = blk_i[:, :].rearrange("p (w k) -> p w k", k=HALF)
                dve.tensor_copy(words_g[:, :], b5[:, :, HALF - 1])
                dve.drain()
                for k in range(HALF - 2, -1, -1):
                    dve.scalar_tensor_tensor(words_g[:, :], words_g[:, :], 6, b5[:, :, k],
                                             ALU.logical_shift_left, ALU.bitwise_or)
                    dve.drain()
                dve.tensor_copy(block_words[:, bass.ds(g * (2 * BODIES) + 2, 2 * BODIES)], words_g[:, :])
                dve.drain().then_inc(s_group, 1)

            dve.wait_ge(s_count, GROUPS + 1)
            dve.tensor_scalar(small[:, 6, 0:NB], deg_ps[:, 0:NB], 1.0, None, ALU.max).then_inc(s_degmax, 1)
            dve.tensor_scalar(small[:, 5, 0:NB], deg_ps[:, 0:NB], 0.0, None, ALU.is_gt)
            dve.wait_ge(s_root, 1)
            dve.reciprocal(small[:, 6, 0:NB], dinv[:, 0:NB])
            dve.drain()
            dve.tensor_tensor(small[:, 7, 0:NB], small[:, 6, 0:NB], small[:, 5, 0:NB], ALU.mult)
            dve.drain().then_inc(s_dinv, 1)

            PART = 3 * SRC_H
            LIST = HALF * (1 + NBASE)
            rec_flat = records[:, :, :, :].rearrange("p b r j -> p (b r j)")
            list_flat = lists[:, :, :].rearrange("p b w -> p (b w)")

            def stage_src(h, part, n8):
                dve.wait_ge(s_rec, n8 + 1)
                dve.tensor_copy(src_now[:, h, :, :].rearrange("p r j -> p (r j)"),
                                rec_flat[:, bass.ds(part * PART, PART)]).then_inc(s_src, 1)

            def hots_src(n8, n2, j):
                h, at = divmod(j, SRC_H)
                if at == 0:
                    dve.wait_ge(s_src, n2 + (h + 1))
                dve.wait_ge(s_put, n8 + (j + 1))
                dve.tensor_scalar(hot_slot[:, j, :], iota_b[:, :], src_now[:, h, 1, at:at + 1], None, ALU.is_equal)
                dve.tensor_scalar(hot_tile[:, j, :], iota_f[:, 0:TILES], src_now[:, h, 0, at:at + 1],
                                  src_now[:, h, 2, at:at + 1], ALU.is_equal, ALU.mult).then_inc(s_rec, 1)

            def decode(g):
                dve.wait_ge(s_sorted, g + 1)
                dve.wait_ge(s_actidle, g + 1)
                halves = sorted_ps[:, 0:2 * TILES].bitcast(I32).rearrange("p (t h) -> p t h", h=2)
                dve.tensor_scalar(idx_all[:, 0:TILES], halves[:, :, 1], 16, LOW13, ALU.logical_shift_right, ALU.bitwise_and)
                dve.tensor_scalar(tmp_a[:, 0:TILES], halves[:, :, 0], 22, None, ALU.logical_shift_right)
                dve.tensor_scalar(tmp_b[:, 0:TILES], halves[:, :, 0], 16, 63, ALU.logical_shift_right, ALU.bitwise_and)
                dve.drain()
                dve.tensor_copy(lists[:, 0:2 * BODIES, 0:HALF], tmp_a[:, 0:TILES].rearrange("p (h t) -> p h t", t=HALF))
                dve.tensor_copy(type_b[:, :], tmp_b[:, 0:TILES])
                dve.drain().then_inc(s_decode, 1)
                dve.wait_ge(s_typet, g + 1)
                dve.tensor_copy(type_t[0:PAIRS, :, :], type_ps[0:PAIRS, :].rearrange("p (h s) -> p h s", h=2)).then_inc(s_typec, 1)
                dve.wait_ge(s_typein, g * 32 + 32)
                dve.tensor_scalar(type_hot[:, :], type_hot[:, :], pcol[:, 1:2], None, ALU.is_equal).then_inc(s_typehot, 1)
                dve.wait_ge(s_w, g + 1)

            def stage_list(h, part, n10):
                dve.wait_ge(s_wb, n10 + TILE_U)
                dve.tensor_copy(list_now[:, h, :], list_flat[:, bass.ds(part * LIST, LIST)]).then_inc(s_list, 1)

            def hots_tile(n51, k):
                h, t = divmod(k, HALF)
                if t == 0:
                    dve.wait_ge(s_list, n51 + (h + 1))
                o = k * NBASE * D
                at = HALF + t * NBASE
                dve.tensor_scalar(wb[:, o:o + D], iota_mark[:, :], list_now[:, h, t:t + 1], list_now[:, h, at:at + 1],
                                  ALU.is_equal, ALU.mult)
                dve.tensor_scalar(hot_row[:, k * D:(k + 1) * D], iota_mark[:, :], list_now[:, h, t:t + 1], None,
                                  ALU.is_equal).then_inc(s_row, 1)

            def add_tile(n10, k, word):
                at = 6 * (k % HALF) - 7
                off = word & (63 << 6 * (k % HALF))
                off = (off >> at) if at >= 0 else (off << -at)
                off = dve.snap(off, min_val=0, max_val=NB * D)
                dst_ap = block_sum[:, bass.ds(off, D)]
                dve.wait_ge(s_sum, n10 + (1 + TILE_U - HALF))
                dve.wait_ge(s_acc, n10 + 1)
                dve.tensor_tensor(dst_ap, tile_sum(k), dst_ap, ALU.add).then_inc(s_acc, 1)

            def word_at(part):
                return dve.value_load(block_words[0:1, bass.ds(part, 1)], min_val=0, max_val=(1 << 30) - 1)

            def main(g, with_sort):
                with dve.Fori(0, BODIES) as i:
                    n10 = dve.snap(i * TILE_U + g * TILES)
                    n8 = dve.snap(i * SRC_U + (g + 1) * SRC_G)
                    n2 = i * 2 + (g + 1) * (2 * BODIES + 1)
                    n51 = i * 2 + g * (2 * BODIES + 1)
                    part = i * 2 + g * (2 * BODIES)
                    for k in range(TILE_U):
                        if k % HALF == 0:
                            word = word_at(part + (1 + k // HALF))
                        add_tile(n10 + k, (k + HALF) % TILE_U, word)
                        hots_tile(n51, k)
                        if with_sort and k in SRC_AT:
                            hots_src(n8, n2, SRC_AT.index(k))
                        if k == STAGE_AT[0]:
                            stage_list(1, i * 2 + 1, n10)
                            if with_sort:
                                stage_src(1, part + (2 * BODIES + 1), n8)
                        if k == STAGE_AT[1]:
                            stage_list(0, i * 2 + 2, n10 + HALF)
                            if with_sort:
                                stage_src(0, part + (2 * BODIES + 2), n8 + SRC_H)

            stage_src(0, 0, 0)
            with dve.Fori(0, BODIES) as i:
                for j in range(SRC_U):
                    if j == 1:
                        stage_src(1, i * 2 + 1, i * SRC_U)
                    hots_src(i * SRC_U, i * 2, j)
                    if j == SRC_H + 1:
                        stage_src(0, i * 2 + 2, i * SRC_U + SRC_H)
            dve.wait_ge(s_clear, 1)
            with dve.Fori(0, GROUPS - 1) as g:
                decode(g)
                stage_src(0, g * (2 * BODIES) + 2 * BODIES, (g + 1) * SRC_G)
                stage_list(0, 0, g * TILES)
                main(g, True)
            g = GROUPS - 1
            decode(g)
            stage_list(0, 0, g * TILES)
            main(g, False)
            word = word_at(2 * GROUPS * BODIES + 1)
            for k in range(HALF):
                add_tile(GROUPS * TILES + k, HALF + k, word)
            dve.drain()

            sums = block_sum[:, 0:NB * D].rearrange("p (j d) -> p j d", d=D)
            dve.tensor_tensor(sums, sums, inner(small[:, 7, 0:NB], D), ALU.mult)
            dve.drain()
            dve.tensor_tensor(x_sb[:, 0:NB, :], x_sb[:, 0:NB, :], sums, ALU.add)
            dve.drain()
            dve.tensor_reduce(stat[:, 2, 0:NB], x_sb[:, 0:NB, :], AX.X, ALU.add)
            dve.drain()
            dve.tensor_scalar(stat[:, 2, 0:NB], stat[:, 2, 0:NB], 1.0 / D, None, ALU.mult)
            dve.drain()
            dve.tensor_tensor(x_sb[:, 0:NB, :], x_sb[:, 0:NB, :], inner(stat[:, 2, 0:NB], D), ALU.subtract)
            dve.drain().then_inc(s_fin, 1)
            dve.wait_ge(s_sq, 1)
            dve.tensor_reduce(stat[:, 0, 0:NB], sums, AX.X, ALU.add)
            dve.drain()
            dve.tensor_scalar(stat[:, 0, 0:NB], stat[:, 0, 0:NB], 1.0 / D, 1e-5, ALU.mult, ALU.add)
            dve.drain().then_inc(s_var, 1)
            dve.wait_ge(s_std, 1)
            dve.reciprocal(stat[:, 3, 0:NB], stat[:, 1, 0:NB])
            dve.drain()
            for c in range(NB // 7):
                j = slice(7 * c, 7 * c + 7)
                dve.tensor_tensor(x_sb[:, j, :], x_sb[:, j, :], inner(stat[:, 3, j], D), ALU.mult).then_inc(s_outr, 1)


def kernel(x, src, dst, edge_type_50, L0_gnn_bases, L0_gnn_comps, L0_gnn_alpha):
    import numpy as np
    import concourse.bacc as bacc
    from concourse.bass_utils import run_bass_kernel_spmd

    given = dict(x=x, src=src, dst=dst, etype=edge_type_50, bases=L0_gnn_bases, comps=L0_gnn_comps, alpha=L0_gnn_alpha)
    arrays = {name: np.ascontiguousarray(a) for name, a in given.items()}
    nc = bacc.Bacc("TRN2", target_bir_lowering=False, num_devices=1)
    aps = {name: nc.dram_tensor(name, a.shape, mybir.dt.from_np(a.dtype), kind="ExternalInput").ap()
           for name, a in arrays.items()}
    out = nc.dram_tensor("out", arrays["x"].shape, F32, kind="ExternalOutput").ap()
    relational_layer(nc, **aps, out=out)
    r = run_bass_kernel_spmd(nc, [arrays], core_ids=[0])
    return r.results[0]["out"]
```

```python
from contextlib import ExitStack

import concourse.bass as bass
from concourse import mybir

ALU = mybir.AluOpType
ACT = mybir.ActivationFunctionType
AX = mybir.AxisListType
F32 = mybir.dt.float32
BF16 = mybir.dt.bfloat16
I32 = mybir.dt.int32

P = 128
GROUPS = 4
BODIES = 25
TILE_U = 10
SRC_U = 10
SORTING = 20
HALF = TILE_U // 2
SRC_H = SRC_U // 2
READ_AT, TURN_AT, COPY_AT = 2, 4, 6
WEIGH_AT = (17, 25, 33, 41)
SPREAD_AT = (8, 16, 24, 32)
INDEX_AT = 7
ALL_BY_ACT = (1, 6)
WEIGHTS_AT = (0, 1, 4, 5)
STAGE_AT = (2, 7)
MARK = 0x2000
LOW13 = MARK - 1


def relational_layer(nc, x, src, dst, etype, bases, comps, alpha, out):
    N, D = x.shape
    E = src.shape[0]
    NBASE = bases.shape[0]
    NREL = comps.shape[0]
    ZW = NBASE * D
    NB = (N + P - 1) // P
    TAIL = N - (NB - 1) * P
    COLS = (E + P - 1) // P
    LASTC = E - (P - 1) * COLS
    SRC_G = SORTING * SRC_U
    TILES = BODIES * TILE_U
    ALLC = GROUPS * SRC_G
    PAIRS = TILES // 2
    QUARTER = (PAIRS + 3) // 4
    SORT_B = 10
    SORT_C = 4 * SORT_B
    CH = 7
    CH_DVE = 4
    FIRSTS = 6
    ZB = 5 * SORT_B
    YB = ZB + 2
    assert D == P and N <= MARK and NREL <= 64 and NB <= min(63, ZB) and YB <= 64
    assert (QUARTER * 2) % 64 == 0 and NB % CH == 0 and ALLC >= COLS
    assert 2 * TILES <= 512 and SRC_G * SORT_B == ZB * SORT_C
    assert SRC_G <= 256
    assert (SRC_G * P + NB * (P - 1)) // P <= TILES

    with ExitStack() as ctx:
        def sb(name, shape, dt):
            return ctx.enter_context(nc.sbuf_tensor(name, shape, dt))

        def sem(name):
            return ctx.enter_context(nc.semaphore(name))

        z_table = nc.dram_tensor("z_table", (ZB * P, ZW), F32).ap()
        type_rows = nc.dram_tensor("type_rows", (2, PAIRS, P), BF16).ap()

        x_sb = sb("x_sb", [P, YB, D], F32)
        HOTS = NB * SRC_G // 2
        big = sb("big", [P, max(2 * HOTS, PAIRS * P // 2)], F32)
        hot_blk = [big[:, b * HOTS:(b + 1) * HOTS].bitcast(BF16) for b in range(2)]
        type_hot = big[:, 0:PAIRS * P // 2].bitcast(BF16)
        SUMW = 64 * D
        arena = sb("arena", [P, SUMW + TILE_U * NBASE * D], F32)
        hot_low = arena[:, 0:P * SRC_G // 2].bitcast(BF16)
        block_sum = arena[:, 0:SUMW]
        work = arena[:, SUMW:]
        y_ring = work[:, 0:2 * D]
        yt_ring = work[:, 2 * D:4 * D]
        wb = work[:, 0:TILE_U * NBASE * D]
        z_ring = sb("z_ring", [P, TILE_U, ZW], F32)
        z_flat = z_ring[:, :, :].rearrange("p a d -> p (a d)")
        src_i, dst_i, typ_i, low_i, hi_i = (z_flat[:, r * ALLC:(r + 1) * ALLC].bitcast(I32) for r in range(5))
        running = z_flat[:, 0:HOTS].bitcast(BF16)
        hot_row = sb("hot_row", [P, TILE_U * D], BF16)
        hi_b = sb("hi_b", [P, ALLC], BF16)
        lo_b = sb("lo_b", [P, ALLC], BF16)
        hi_g = sb("hi_g", [P, SRC_G], BF16)
        lo_g = sb("lo_g", [P, SRC_G], BF16)
        records = sb("records", [P, ALLC // SRC_H + 2, 3, SRC_H], F32)
        idx_all = sb("idx_all", [P, GROUPS * TILES + 2 * TILE_U], I32)
        lists = sb("lists", [P, GROUPS * 2 * BODIES + 1, HALF * (1 + NBASE)], F32)
        tmp_a = sb("tmp_a", [P, 256], I32)
        tmp_b = sb("tmp_b", [P, 256], I32)
        type_b = sb("type_b", [P, TILES], BF16)
        type_t = sb("type_t", [P, 2, P], BF16)
        block_words = sb("block_words", [1, 2 + GROUPS * 2 * BODIES], I32)
        words_g = sb("words_g", [1, 2 * BODIES], I32)
        blk_i = sb("blk_i", [1, TILES], I32)
        hot_slot = sb("hot_slot", [P, SRC_U, P], F32)
        first_of = hot_slot[:, :, :].rearrange("p a b -> p (a b)")[:, 0:FIRSTS * SRC_G].rearrange(
            "p (r c) -> p r c", c=SRC_G)
        hot_tile = sb("hot_tile", [P, SRC_U, TILES], BF16)
        src_now = sb("src_now", [P, 2, 3, SRC_H], F32)
        list_now = sb("list_now", [P, 2, HALF * (1 + NBASE)], F32)
        idx_now = sb("idx_now", [P, 2 * TILE_U], I32)
        bases_sb = sb("bases_sb", [P, NBASE, D], F32)
        iota_i = sb("iota_i", [P, 256], I32)
        pcol_i = sb("pcol_i", [P, 2], I32)
        pcol = sb("pcol", [P, 2], F32)
        iota_f = sb("iota_f", [P, 256], F32)
        iota_h = sb("iota_h", [P, 256], BF16)
        iota_b = sb("iota_b", [P, P], BF16)
        iota_mark = sb("iota_mark", [P, P], BF16)
        ident_f = sb("ident_f", [P, P], F32)
        ident_b = sb("ident_b", [P, P], BF16)
        below = sb("below", [P, P], BF16)
        ones_b = sb("ones_b", [P, SRC_G], BF16)
        zeros_b = sb("zeros_b", [P, 512], BF16)
        w_table = sb("w_table", [P, 2 * NBASE], F32)
        w_rest = sb("w_rest", [P, 2 * NBASE], F32)
        alpha_sb = sb("alpha_sb", [P, 1], F32)
        w_parts = sb("w_parts", [P, 3, 2 * NBASE], BF16)
        small = sb("small", [P, 8, 64], F32)
        small_i = sb("small_i", [P, 64], I32)
        ge = sb("ge", [P, 256], BF16)
        dinv = sb("dinv", [P, 64], F32)
        eps = sb("eps", [P, 1], F32)
        stat = sb("stat", [P, 5, 64], F32)

        bank = [ctx.enter_context(nc.psum_tensor(f"bank{i}", [P, 512], F32)) for i in range(8)]
        SUMS = HALF
        tile_sum = lambda k: bank[k % SUMS][:, 0:D]
        w_ps = [bank[5], bank[6]]
        sorted_ps = bank[7]
        type_ps = bank[5][:, 0:P].bitcast(BF16)
        deg_ps = bank[7]
        turned = lambda k: bank[3 + k][:, 0:D]
        before_ps, total_ps, blk_ps, slot_ps = bank[0], bank[1], bank[2], bank[3]

        s_fill = sem("s_fill")
        s_iota = sem("s_iota")
        s_load = sem("s_load")
        s_x = sem("s_x")
        s_bases = sem("s_bases")
        s_const = sem("s_const")
        s_hot = sem("s_hot")
        s_low = sem("s_low")
        s_deg = sem("s_deg")
        s_base = sem("s_base")
        s_first = sem("s_first")
        s_firstused = sem("s_firstused")
        s_rank = sem("s_rank")
        s_slot = sem("s_slot")
        s_clear = sem("s_clear")
        s_count = sem("s_count")
        s_cut = sem("s_cut")
        s_blk = sem("s_blk")
        s_group = sem("s_group")
        s_degmax = sem("s_degmax")
        s_root = sem("s_root")
        s_dinv = sem("s_dinv")
        s_y = sem("s_y")
        s_yt = sem("s_yt")
        s_ytc = sem("s_ytc")
        s_z = sem("s_z")
        s_zc = sem("s_zc")
        s_zw = [sem(f"s_zw{k}") for k in range(2)]
        s_rec = sem("s_rec")
        s_put = sem("s_put")
        s_sorted = sem("s_sorted")
        s_decode = sem("s_decode")
        s_typet = sem("s_typet")
        s_typec = sem("s_typec")
        s_typeout = sem("s_typeout")
        s_typein = [sem(f"s_typein{q}") for q in range(4)]
        s_typehot = sem("s_typehot")
        s_wps = sem("s_wps")
        s_w = sem("s_w")
        s_idx = sem("s_idx")
        s_gat = [sem(f"s_gat{k}") for k in range(TILE_U)]
        s_begun = sem("s_begun")
        s_row = sem("s_row")
        s_wb = sem("s_wb")
        s_list = sem("s_list")
        s_src = sem("s_src")
        s_sum = sem("s_sum")
        s_acc = sem("s_acc")
        s_fin = sem("s_fin")
        s_std = sem("s_std")
        s_scale = sem("s_scale")
        s_outdve = sem("s_outdve")
        s_outact = sem("s_outact")
        s_out = sem("s_out")

        block = ctx.enter_context(nc.Block())

        def chunk(c):
            return slice(c * CH, (c + 1) * CH)

        def quarter(q):
            return slice(q * QUARTER * P, min(PAIRS, (q + 1) * QUARTER) * P)

        def bc(ap, shape):
            return ap.to_broadcast(shape)

        def inner(ap, n):
            return bc(ap.rearrange("p (a b) -> p a b", b=1), [ap.shape[0], ap.shape[1], n])

        def outer(ap, n):
            return bc(ap.rearrange("p (a b) -> p a b", a=1), [ap.shape[0], n, ap.shape[1]])

        @block.sync
        def _(sp):
            sp.wait_ge(s_fill, 6)
            whole, last = slice(0, (P - 1) * COLS), slice((P - 1) * COLS, E)
            for a, t in ((src, src_i), (dst, dst_i), (etype, typ_i)):
                sp.dma_start(t[0:P - 1, 0:COLS], a[whole].rearrange("(p c) -> p c", c=COLS)).then_inc(s_load, 16)
                sp.dma_start(t[P - 1:P, 0:LASTC], a[last].rearrange("(p c) -> p c", p=1)).then_inc(s_load, 16)
            for h in range(2):
                sp.dma_start(w_table[64 * h:64 * h + NREL, NBASE * h:NBASE * (h + 1)], comps).then_inc(s_load, 16)
                sp.dma_start(alpha_sb[64 * h:64 * h + NREL, :], alpha).then_inc(s_load, 16)
            sp.dma_start(bases_sb[:, :, :], bases.rearrange("b d f -> d b f")).then_inc(s_bases, 16)
            full = (NB - 1) * P
            sp.dma_start(x_sb[:, 0:NB - 1, :], x[0:full, :].rearrange("(j p) d -> p j d", p=P)).then_inc(s_x, 16)
            sp.dma_start(x_sb[0:TAIL, NB - 1, :], x[full:N, :]).then_inc(s_x, 16)

            with sp.Fori(0, ZB // 2) as i:
                for k in range(2):
                    sp.wait_ge(s_zc, i * 2 + (k + 3))
                    sp.dma_start(z_table[bass.ds(i * (2 * P) + k * P, P), :], z_ring[:, k, :]).then_inc(s_zw[k], 16)

            def spread_types(g, started):
                sp.wait_ge(s_typec, g + 1)
                sp.dma_start(type_rows.rearrange("h i s -> i h s"), type_t[0:PAIRS, :, :]).then_inc(s_typeout, 16)
                sp.wait_ge(s_typeout, g * 16 + 16)
                for q in range(4):
                    if started:
                        sp.wait_ge(s_sum, g * TILES + (SORTING * TILE_U + SPREAD_AT[q] + TILE_U - TILES))
                    for h in range(2):
                        sp.dma_start(type_hot[64 * h:64 * h + NREL, quarter(q)],
                                     bc(type_rows[h:h + 1, :, :].rearrange("h i s -> h (i s)")[:, quarter(q)],
                                        [NREL, quarter(q).stop - quarter(q).start])).then_inc(s_typein[q], 16)

            spread_types(0, False)
            with sp.Fori(1, GROUPS) as g:
                spread_types(g, True)

            for c in range(NB // CH):
                for made, j0, j1 in ((s_outdve, 0, CH_DVE), (s_outact, CH_DVE, CH)):
                    sp.wait_ge(made, c + 1)
                    j0, j1 = j0 + c * CH, j1 + c * CH
                    whole = min(j1, NB - 1)
                    sp.dma_start(out[j0 * P:whole * P, :].rearrange("(j p) d -> p j d", p=P),
                                 x_sb[:, j0:whole, :]).then_inc(s_out, 16)
            sp.dma_start(out[(NB - 1) * P:N, :], x_sb[0:TAIL, NB - 1, :]).then_inc(s_out, 16)
            sp.wait_ge(s_out, 16 * (2 * (NB // CH) + 1))

        @block.gpsimd
        def _(pool):
            pool.memset(src_i, NB * P).then_inc(s_fill, 1)
            pool.memset(dst_i, 0).then_inc(s_fill, 1)
            pool.memset(typ_i, 0).then_inc(s_fill, 1)
            pool.memset(w_table[:, :], 0.0).then_inc(s_fill, 1)
            pool.memset(alpha_sb[:, :], 0.0).then_inc(s_fill, 1)
            pool.memset(x_sb[:, NB - 1:YB, :].rearrange("p j d -> p (j d)"), 0.0).then_inc(s_fill, 1)
            pool.iota(iota_i[:, :], [[1, 256]], base=0, channel_multiplier=0).then_inc(s_iota, 1)
            pool.iota(pcol_i[:, 0:1], [[1, 1]], base=0, channel_multiplier=1).then_inc(s_iota, 1)
            pool.memset(ones_b[:, :], 1.0).then_inc(s_iota, 1)
            pool.memset(zeros_b[:, :], 0.0).then_inc(s_iota, 1)
            pool.memset(lists[:, GROUPS * 2 * BODIES, :], 0.0).then_inc(s_iota, 1)
            pool.memset(records[:, :, :, :], 0.0).then_inc(s_iota, 1)
            pool.memset(idx_all[:, GROUPS * TILES:], 0).then_inc(s_iota, 1)
            pool.wait_ge(s_deg, GROUPS + 2)
            pool.memset(block_sum, 0.0).then_inc(s_clear, 1)
            for k in range(2):
                pool.wait_ge(s_zw[k], 16 * (ZB // 2) + 16)
            pool.wait_ge(s_idx, 2)
            with pool.Fori(0, GROUPS * BODIES // 4) as i:
                done = pool.snap(i * (4 * TILE_U))
                for t in range(4 * TILE_U):
                    k = t % TILE_U
                    if t % 2 == 0:
                        pool.wait_ge(s_sum, done + (t + 2))
                        pool.sem_inc(s_begun, 1)
                    pool.indirect_dma_start(
                        out=z_ring[:, k, :], out_offset=None, in_=z_table,
                        in_offset=bass.IndirectOffsetOnAxis(ap=idx_now[:, t % (2 * TILE_U):t % (2 * TILE_U) + 1], axis=0),
                    ).then_inc(s_gat[k], 16)

        @block.scalar
        def _(act):
            act.sem_inc(s_ytc, 2)
            act.sem_inc(s_zc, 2)
            for k in range(2):
                act.sem_inc(s_zw[k], 16)
            act.sem_inc(s_wb, TILE_U)
            with act.Fori(0, GROUPS // 2) as i:
                for b in range(2):
                    g = i * 2 + b
                    act.wait_ge(s_base, g + 1)
                    for j in range(NB):
                        act.wait_ge(s_firstused, g * NB + (j + 1))
                        act.activation(first_of[:, j % FIRSTS, :], hot_blk[b][:, j * SRC_G:(j + 1) * SRC_G], ACT.Copy,
                                       scale=small[:, 4, j:j + 1]).then_inc(s_first, 1)
            act.wait_ge(s_degmax, 1)
            act.activation(dinv[:, 0:NB], small[:, 6, 0:NB], ACT.Sqrt).then_inc(s_root, 1)
            act.wait_ge(s_dinv, 1)
            act.wait_ge(s_x, 32)
            x_flat = x_sb[:, :, :].rearrange("p j d -> p (j d)")

            def scale(n, k):
                act.activation(y_ring[:, k * D:(k + 1) * D], x_flat[:, bass.ds(n * D, D)], ACT.Copy,
                               scale=small[:, 7, bass.ds(n, 1)]).then_inc(s_y, 1)

            def copy_turned(n, k):
                act.wait_ge(s_yt, n + 1)
                act.activation(yt_ring[:, k * D:(k + 1) * D], turned(k), ACT.Copy).then_inc(s_ytc, 1)

            scale(0, 0)
            scale(1, 1)
            copy_turned(0, 0)
            with act.Fori(0, ZB // 2) as i:
                for k in range(2):
                    n = act.snap(i * 2 + k)
                    copy_turned(n + 1, 1 - k)
                    scale(n + 2, k)
                    act.wait_ge(s_z, n + 1)
                    act.wait_ge(s_zw[k], i * 16 + 16)
                    act.activation(z_ring[:, k, :], bank[k][:, :], ACT.Copy).then_inc(s_zc, 1)

            full, cut = divmod(128, HALF)
            halves = 2 * BODIES

            def weights(piece, g):
                h0, h1, t0, t1, w = (
                    (0, full, 0, HALF, w_ps[0][:, 0:full * HALF * NBASE]),
                    (full, full + 1, 0, cut, w_ps[0][:, full * HALF * NBASE:128 * NBASE]),
                    (full, full + 1, cut, HALF, w_ps[1][:, 0:(HALF - cut) * NBASE]),
                    (full + 1, halves, 0, HALF, w_ps[1][:, (HALF - cut) * NBASE:(TILES - 128) * NBASE]))[piece]
                act.activation(lists[:, bass.ds(g * halves + h0, h1 - h0), HALF + t0 * NBASE:HALF + t1 * NBASE],
                               w.rearrange("p (h w) -> p h w", h=h1 - h0), ACT.Copy).then_inc(s_w, 1)

            def stage_idx(n, half):
                return act.activation(idx_now[:, bass.ds(half * TILE_U, TILE_U)],
                                      idx_all[:, bass.ds(n * TILE_U, TILE_U)], ACT.Copy)

            def tiles(n, decoded=None, g=None):
                n10 = act.snap(n * TILE_U)
                for k in range(TILE_U):
                    act.wait_ge(s_row, n10 + (k + 1))
                    for b in range(0 if k in ALL_BY_ACT else 1, NBASE):
                        o = (k * NBASE + b) * D
                        at = HALF + (k % HALF) * NBASE + b
                        last = act.activation(wb[:, o:o + D], hot_row[:, k * D:(k + 1) * D], ACT.Copy,
                                              scale=list_now[:, k // HALF, at:at + 1])
                    last.then_inc(s_wb, 1)
                    if k == INDEX_AT:
                        act.wait_ge(s_gat[TILE_U - 1], n * 16 + 16)
                        if decoded is not None:
                            act.wait_ge(s_decode, decoded + 1)
                        stage_idx(n + 2, n & 1)
                    if g is not None and k in WEIGHTS_AT:
                        piece = WEIGHTS_AT.index(k)
                        act.wait_ge(s_wps, g * 2 + (1 + piece // 2))
                        weights(piece, g)

            act.wait_ge(s_decode, 1)
            for n in range(2):
                stage_idx(n, n).then_inc(s_idx, 1)
            act.wait_ge(s_wps, 2)
            for piece in range(4):
                weights(piece, 0)
            with act.Fori(0, GROUPS - 1) as g:
                with act.Fori(0, BODIES - 2) as i:
                    tiles(g * BODIES + i)
                tiles(g * BODIES + (BODIES - 2), decoded=g + 1)
                tiles(g * BODIES + (BODIES - 1), g=g + 1)
            with act.Fori((GROUPS - 1) * BODIES, GROUPS * BODIES) as i:
                tiles(i)

            for c in range(NB // CH + 2):
                if c < NB // CH:
                    act.wait_ge(s_fin, c + 1)
                    for j in range(c * CH, (c + 1) * CH):
                        act.activation(block_sum[:, j * D:(j + 1) * D], x_sb[:, j, :], ACT.Square,
                                       bias=stat[:, 2, j:j + 1], accum_out=stat[:, 0, j:j + 1])
                    act.drain()
                    act.activation(stat[:, 1, chunk(c)], stat[:, 0, chunk(c)], ACT.Sqrt, scale=1.0 / D,
                                   bias=eps[:, 0:1]).then_inc(s_std, 1)
                if c >= 2:
                    act.wait_ge(s_scale, c - 1)
                    for j in range((c - 2) * CH + CH_DVE, (c - 1) * CH):
                        last = act.activation(x_sb[:, j, :], x_sb[:, j, :], ACT.Identity, scale=stat[:, 3, j:j + 1],
                                              bias=stat[:, 4, j:j + 1])
                    last.then_inc(s_outact, 1)

        @block.tensor
        def _(pe):
            pe.sem_inc(s_deg, 2)
            pe.sem_inc(s_firstused, FIRSTS)
            pe.sem_inc(s_put, SRC_U)
            pe.sem_inc(s_sum, TILE_U)
            pe.wait_ge(s_const, 1)
            pe.matmul(deg_ps[:, 0:NB], zeros_b[:, 0:P], zeros_b[:, 0:NB], start=True, stop=False, skip_group_check=True)
            low_rc = hot_low.rearrange("p (r c) -> p r c", c=SRC_G)

            def count(g, hot_jc):
                pe.wait_ge(s_hot, g + 1)
                for c in range(0, SRC_G, 10):
                    part = hot_jc[:, :, c:c + 10]
                    ends = dict(start=(c == 0), stop=(c == SRC_G - 10))
                    pe.matmul(before_ps[:, 0:10 * NB].rearrange("p (j r) -> p j r", r=10), below[:, :], part, **ends)
                    last = pe.matmul(total_ps[:, 0:10 * NB].rearrange("p (j r) -> p j r", r=10), ones_b[:, 0:P], part, **ends)
                last.then_inc(s_count, 1)
                pe.wait_ge(s_cut, g + 1)
                pe.matmul(blk_ps[:, 0:TILES], ones_b[:, 0:P], ge[:, 0:TILES], start=True, stop=True).then_inc(s_blk, 1)
                for j in range(NB):
                    pe.wait_ge(s_first, g * NB + (j + 1))
                    pe.matmul(slot_ps[:, 0:SRC_G], ident_f[:, :], first_of[:, j % FIRSTS, :],
                              start=(j == 0), stop=False).then_inc(s_firstused, 1)
                pe.wait_ge(s_rank, g + 1)
                for j in range(NB):
                    last = pe.matmul(slot_ps[:, 0:SRC_G], ident_b[:, :], running[:, j * SRC_G:(j + 1) * SRC_G],
                                     start=False, stop=(j == NB - 1))
                last.then_inc(s_slot, 1)
                pe.wait_ge(s_low, g + 1)
                for c in range(SRC_G):
                    last = pe.matmul(deg_ps[:, 0:NB], low_rc[:, :, c], hot_jc[:, :, c],
                                     start=False, stop=False, skip_group_check=True)
                last.then_inc(s_deg, 1)
            with pe.Fori(0, GROUPS // 2) as i:
                for b in range(2):
                    count(i * 2 + b, hot_blk[b].rearrange("p (j c) -> p j c", c=SRC_G))
            pe.matmul(deg_ps[:, 0:NB], zeros_b[:, 0:P], zeros_b[:, 0:NB], start=False, stop=True,
                      skip_group_check=True).then_inc(s_count, 1)

            def open_sort():
                pe.matmul(sorted_ps[:, 0:2 * TILES], zeros_b[:, 0:P], zeros_b[:, 0:2 * TILES],
                          start=True, stop=False, skip_group_check=True)

            def put(n, k):
                pe.wait_ge(s_rec, n + 2)
                for h in range(2):
                    last = pe.matmul(sorted_ps[:, h * TILES:(h + 1) * TILES], hot_slot[:, k, :].bitcast(BF16)[:, h::2],
                                     hot_tile[:, k, :], start=False, stop=False, skip_group_check=True)
                last.then_inc(s_put, 1)

            def close_sort():
                pe.matmul(sorted_ps[:, 0:2 * TILES], zeros_b[:, 0:P], zeros_b[:, 0:2 * TILES],
                          start=False, stop=True, skip_group_check=True).then_inc(s_sorted, 1)

            def turn_types(g):
                pe.wait_ge(s_decode, g + 1)
                for h in range(2):
                    last = pe.transpose(type_ps[0:PAIRS, h * P:(h + 1) * P],
                                        type_b[:, h:TILES:2], ident_b[:, :])
                last.then_inc(s_typet, 1)

            def weights(g, q):
                pe.wait_ge(s_typehot, g * 4 + (q + 1))
                for i in range(q * QUARTER, min(PAIRS, (q + 1) * QUARTER)):
                    o = (i % 64) * 2 * NBASE
                    for part in range(3):
                        last = pe.matmul(w_ps[i // 64][:, o:o + 2 * NBASE], type_hot[:, i * P:(i + 1) * P],
                                         w_parts[:, part, :], start=(part == 0), stop=(part == 2))
                if q % 2 == 1:
                    last.then_inc(s_wps, 1)

            def tile(n, k):
                pe.wait_ge(s_wb, n * TILE_U + (k + 1 + TILE_U))
                pe.wait_ge(s_gat[k], n * 16 + 16)
                for b in range(NBASE):
                    o = (k * NBASE + b) * D
                    last = pe.matmul(tile_sum(k), wb[:, o:o + D], z_ring[:, k, b * D:(b + 1) * D],
                                     start=(b == 0), stop=(b == NBASE - 1))
                last.then_inc(s_sum, 1)

            pe.wait_ge(s_bases, 16)
            pe.wait_ge(s_group, GROUPS)
            pe.matmul(bank[2][:, 0:D], zeros_b[:, 0:P], zeros_b[:, 0:D], start=True, stop=True)
            pe.wait_ge(s_dinv, 1)
            open_sort()
            def turn(n, k):
                pe.wait_ge(s_y, n + 1)
                pe.wait_ge(s_ytc, n + 1)
                pe.transpose(turned(k), y_ring[:, k * D:(k + 1) * D], ident_f[:, :]).then_inc(s_yt, 1)

            turn(0, 0)
            with pe.Fori(0, ZB // SORT_B) as i:
                for b in range(SORT_B):
                    k, n = b % 2, i * SORT_B + b
                    c, cn = 4 * b, i * SORT_C + 4 * b
                    turn(n + 1, 1 - k)
                    put(cn, c % SRC_U)
                    put(cn + 1, (c + 1) % SRC_U)
                    pe.wait_ge(s_ytc, n + 3)
                    pe.wait_ge(s_zc, n + 1)
                    pe.matmul(bank[k][:, :], yt_ring[:, k * D:(k + 1) * D],
                              bases_sb[:, :, :].rearrange("p b f -> p (b f)"), start=True, stop=True).then_inc(s_z, 1)
                    put(cn + 2, (c + 2) % SRC_U)
                    put(cn + 3, (c + 3) % SRC_U)
            close_sort()
            pe.wait_ge(s_ytc, ZB + 3)
            pe.wait_ge(s_zc, ZB + 2)
            turn_types(0)
            for q in range(4):
                weights(0, q)
            with pe.Fori(0, GROUPS - 1) as g:
                open_sort()
                with pe.Fori(0, SORTING) as i:
                    for k in range(TILE_U):
                        tile(g * BODIES + i, k)
                        put((g + 1) * SRC_G + i * SRC_U + k, k)
                close_sort()
                for t in range((BODIES - SORTING) * TILE_U):
                    tile(g * BODIES + (SORTING + t // TILE_U), t % TILE_U)
                    if t == TURN_AT:
                        turn_types(g + 1)
                    if t in WEIGH_AT:
                        weights(g + 1, WEIGH_AT.index(t))
            with pe.Fori((GROUPS - 1) * BODIES, GROUPS * BODIES) as i:
                for k in range(TILE_U):
                    tile(i, k)

        @block.vector
        def _(dve):
            dve.sem_inc(s_acc, 1)
            dve.sem_inc(s_rec, 1)

            dve.wait_ge(s_iota, 7)
            dve.tensor_copy(iota_f[:, :], iota_i[:, :])
            dve.tensor_copy(pcol[:, 0:1], pcol_i[:, 0:1])
            dve.tensor_scalar(pcol_i[:, 1:2], pcol_i[:, 0:1], 63, None, ALU.bitwise_and)
            dve.drain()
            dve.tensor_copy(pcol[:, 1:2], pcol_i[:, 1:2])
            dve.tensor_copy(iota_b[:, :], iota_f[:, 0:P])
            dve.tensor_copy(iota_h[:, :], iota_f[:, :])
            dve.tensor_copy(iota_mark[:, :], iota_f[:, P:2 * P])
            dve.tensor_scalar(ident_f[:, :], iota_f[:, 0:P], pcol[:, 0:1], None, ALU.is_equal)
            dve.tensor_scalar(ident_b[:, :], iota_f[:, 0:P], pcol[:, 0:1], None, ALU.is_equal)
            dve.tensor_scalar(below[:, :], iota_f[:, 0:P], pcol[:, 0:1], None, ALU.is_gt)
            dve.memset(ge[:, :], 0.0)
            dve.memset(eps[:, :], 1e-5)
            dve.drain().then_inc(s_const, 1)

            dve.wait_ge(s_load, 16 * 10)
            dve.tensor_scalar(w_table[:, :], w_table[:, :], alpha_sb[:, 0:1], None, ALU.mult)
            dve.drain()
            for part in range(3):
                dve.tensor_copy(w_parts[:, part, :], w_table[:, :])
                dve.drain()
                if part < 2:
                    dve.tensor_copy(w_rest[:, :], w_parts[:, part, :])
                    dve.drain()
                    dve.tensor_tensor(w_table[:, :], w_table[:, :], w_rest[:, :], ALU.subtract)
                    dve.drain()

            dve.tensor_scalar(typ_i, typ_i, 63, None, ALU.bitwise_and)
            dve.drain()
            dve.tensor_scalar(low_i, src_i, P - 1, None, ALU.bitwise_and)
            dve.tensor_scalar(hi_i, src_i, 7, None, ALU.logical_shift_right)
            dve.drain()
            dve.tensor_copy(lo_b[:, :], low_i)
            dve.tensor_copy(hi_b[:, :], hi_i)
            dve.tensor_scalar(low_i, low_i, 6, None, ALU.logical_shift_left)
            dve.tensor_scalar(dst_i, dst_i, 16, (MARK << 16) | MARK, ALU.logical_shift_left, ALU.bitwise_or)
            dve.drain()
            dve.tensor_tensor(low_i, low_i, typ_i, ALU.bitwise_or)
            dve.drain()
            dve.tensor_tensor(dst_i, dst_i, low_i, ALU.bitwise_or)
            dve.drain()

            rec_i = records[:, :, 2, :].bitcast(I32)

            def put_records(parts, c0, c1):
                while c0 < c1:
                    b0, j0 = divmod(c0, SRC_H)
                    whole = (c1 - c0) // SRC_H * SRC_H if j0 == 0 else 0
                    n = whole or min(SRC_H - j0, c1 - c0)
                    dve.tensor_copy(rec_i[0:parts, b0:b0 + max(1, n // SRC_H), j0:j0 + min(n, SRC_H)],
                                    dst_i[0:parts, c0:c0 + n].rearrange("p (b j) -> p b j", j=min(n, SRC_H)))
                    c0 += n

            put_records(P, 0, LASTC)
            put_records(P - 1, LASTC, COLS)
            dve.drain()

            dve.memset(block_words[:, 0:2], NB)
            dve.drain()
            for _ in range(HALF - 1):
                dve.tensor_scalar(block_words[:, 0:2], block_words[:, 0:2], 6, NB, ALU.logical_shift_left, ALU.bitwise_or)
                dve.drain()
            dve.memset(small[:, 7, :], 0.0)

            before, total, tiles_n, ends, base, endcol = (small[:, r, 0:NB] for r in range(6))
            def hots_blocks(g, b):
                dve.wait_ge(s_deg, g + 1)
                dve.tensor_copy(hi_g[:, :], hi_b[:, bass.ds(g * SRC_G, SRC_G)])
                dve.drain()
                for j in range(NB):
                    dve.tensor_scalar(hot_blk[b][:, j * SRC_G:(j + 1) * SRC_G], hi_g[:, :], float(j), None, ALU.is_equal)
                dve.drain().then_inc(s_hot, 1)

            def slots(g, b):
                dve.tensor_tensor_scan(running, ones_b[:, 0:1].to_broadcast([P, NB * SRC_G]), hot_blk[b], 0.0, ALU.mult, ALU.add)
                dve.tensor_copy(lo_g[:, :], lo_b[:, bass.ds(g * SRC_G, SRC_G)])
                dve.wait_ge(s_count, g + 1)
                for ps, to in ((before_ps, before), (total_ps, total)):
                    dve.tensor_reduce(to, ps[:, 0:10 * NB].rearrange("p (j r) -> p j r", r=10), AX.X, ALU.add)
                dve.drain()
                si = small_i[:, 0:NB]
                dve.tensor_scalar(si, total, float(P - 1), None, ALU.add)
                dve.drain()
                dve.tensor_scalar(si, si, 7, None, ALU.logical_shift_right)
                dve.drain()
                dve.tensor_copy(tiles_n, si)
                dve.drain()
                dve.tensor_tensor_scan(ends, ones_b[:, 0:NB], tiles_n, 0.0, ALU.mult, ALU.add)
                dve.drain()
                dve.tensor_tensor(base, ends, tiles_n, ALU.subtract)
                dve.tensor_tensor(small[0:NB, 6, 0:NB], ends[0:NB, :], ident_f[0:NB, 0:NB], ALU.mult)
                dve.drain()
                dve.tensor_scalar(base, base, float(P), -1.0, ALU.mult, ALU.add)
                dve.tensor_reduce(endcol[0:NB, 0:1], small[0:NB, 6, 0:NB], AX.X, ALU.add)
                dve.drain()
                dve.tensor_tensor(base, base, before, ALU.add)
                dve.drain()
                dve.tensor_tensor(base[:, 1:NB], base[:, 1:NB], running[:, SRC_G - 1:(NB - 1) * SRC_G:SRC_G], ALU.subtract)
                dve.drain().then_inc(s_base, 1)
                dve.tensor_scalar(ge[0:NB, 0:TILES], iota_f[0:NB, 0:TILES], endcol[0:NB, 0:1], None, ALU.is_ge).then_inc(s_cut, 1)
                dve.drain()
                dve.tensor_tensor(running, running, hot_blk[b], ALU.mult).then_inc(s_rank, 1)
                dve.wait_ge(s_deg, g + 2)
                for row in range(P):
                    dve.tensor_scalar(hot_low[:, row * SRC_G:(row + 1) * SRC_G], lo_g[:, :], float(row), None, ALU.is_equal)
                dve.drain().then_inc(s_low, 1)

            def put_slots(g):
                dve.wait_ge(s_slot, g + 1)
                dve.tensor_copy(tmp_b[:, 0:SRC_G], slot_ps[:, 0:SRC_G])
                dve.drain()
                dve.tensor_scalar(tmp_a[:, 0:SRC_G], tmp_b[:, 0:SRC_G], 7, None, ALU.logical_shift_right)
                dve.tensor_scalar(tmp_b[:, 0:SRC_G], tmp_b[:, 0:SRC_G], P - 1, None, ALU.bitwise_and)
                dve.drain()
                for r, t in ((0, tmp_a), (1, tmp_b)):
                    dve.tensor_copy(records[:, bass.ds(g * (SRC_G // SRC_H), SRC_G // SRC_H), r, :],
                                    t[:, 0:SRC_G].rearrange("p (b j) -> p b j", j=SRC_H))
                dve.wait_ge(s_blk, g + 1)
                dve.tensor_copy(blk_i[:, :], blk_ps[0:1, 0:TILES])
                dve.drain()
                b5 = blk_i[:, :].rearrange("p (w k) -> p w k", k=HALF)
                dve.tensor_copy(words_g[:, :], b5[:, :, HALF - 1])
                dve.drain()
                for k in range(HALF - 2, -1, -1):
                    dve.scalar_tensor_tensor(words_g[:, :], words_g[:, :], 6, b5[:, :, k],
                                             ALU.logical_shift_left, ALU.bitwise_or)
                    dve.drain()
                dve.tensor_copy(block_words[:, bass.ds(g * (2 * BODIES) + 2, 2 * BODIES)], words_g[:, :])
                dve.drain().then_inc(s_group, 1)

            with dve.Fori(0, GROUPS // 2) as i:
                hots_blocks(i * 2, 0)
                slots(i * 2, 0)
                hots_blocks(i * 2 + 1, 1)
                put_slots(i * 2)
                slots(i * 2 + 1, 1)
                put_slots(i * 2 + 1)

            dve.wait_ge(s_count, GROUPS + 1)
            dve.tensor_scalar(small[:, 6, 0:NB], deg_ps[:, 0:NB], 1.0, None, ALU.max).then_inc(s_degmax, 1)
            dve.tensor_scalar(small[:, 5, 0:NB], deg_ps[:, 0:NB], 0.0, None, ALU.is_gt)
            dve.wait_ge(s_root, 1)
            dve.reciprocal(small[:, 6, 0:NB], dinv[:, 0:NB])
            dve.drain()
            dve.tensor_tensor(small[:, 7, 0:NB], small[:, 6, 0:NB], small[:, 5, 0:NB], ALU.mult)
            dve.drain().then_inc(s_dinv, 1)

            PART = 3 * SRC_H
            LIST = HALF * (1 + NBASE)
            rec_flat = records[:, :, :, :].rearrange("p b r j -> p (b r j)")
            list_flat = lists[:, :, :].rearrange("p b w -> p (b w)")

            def stage_src(h, part):
                dve.wait_ge(s_rec, part * SRC_H - SRC_H + 1)
                dve.tensor_copy(src_now[:, h, :, :].rearrange("p r j -> p (r j)"),
                                rec_flat[:, bass.ds(part * PART, PART)]).then_inc(s_src, 1)

            def hots_src(n, k):
                h, at = divmod(k, SRC_H)
                if at == 0:
                    dve.wait_ge(s_put, n + SRC_H)
                dve.tensor_scalar(hot_slot[:, k, :], iota_b[:, :], src_now[:, h, 1, at:at + 1],
                                  src_now[:, h, 2, at:at + 1], ALU.is_equal, ALU.mult)
                dve.tensor_scalar(hot_tile[:, k, :], iota_h[:, 0:TILES], src_now[:, h, 0, at:at + 1], None,
                                  ALU.is_equal).then_inc(s_rec, 1)

            def read_records(g):
                dve.wait_ge(s_sorted, g + 1)
                low_half, high_half = (sorted_ps[:, h * TILES:(h + 1) * TILES].bitcast(I32) for h in range(2))
                dve.tensor_scalar(idx_all[:, bass.ds(g * TILES, TILES)], high_half, 16, LOW13, ALU.logical_shift_right, ALU.bitwise_and)
                dve.tensor_scalar(tmp_a[:, 0:TILES], low_half, 22, None, ALU.logical_shift_right)
                dve.tensor_scalar(tmp_b[:, 0:TILES], low_half, 16, 63, ALU.logical_shift_right, ALU.bitwise_and)
                dve.drain()
                dve.tensor_copy(lists[:, bass.ds(g * (2 * BODIES), 2 * BODIES), 0:HALF],
                                tmp_a[:, 0:TILES].rearrange("p (h t) -> p h t", t=HALF))
                dve.tensor_copy(type_b[:, :], tmp_b[:, 0:TILES])
                dve.drain().then_inc(s_decode, 1)

            def copy_types(g):
                dve.wait_ge(s_typet, g + 1)
                dve.tensor_copy(type_t[0:PAIRS, :, :], type_ps[0:PAIRS, :].rearrange("p (h s) -> p h s", h=2)).then_inc(s_typec, 1)

            def hots_types(g, q):
                dve.wait_ge(s_typein[q], g * 32 + 32)
                part = type_hot[:, quarter(q)]
                dve.tensor_scalar(part, part, pcol[:, 1:2], None, ALU.is_equal).then_inc(s_typehot, 1)

            def stage_list(h, part):
                dve.wait_ge(s_wb, part * HALF - HALF + TILE_U)
                dve.tensor_copy(list_now[:, h, :], list_flat[:, bass.ds(part * LIST, LIST)]).then_inc(s_list, 1)

            def hots_tile(n, k):
                h, t = divmod(k, HALF)
                if t == 0:
                    dve.wait_ge(s_list, n * 2 + (h + 1))
                o = k * NBASE * D
                at = HALF + t * NBASE
                if k not in ALL_BY_ACT:
                    dve.tensor_scalar(wb[:, o:o + D], iota_mark[:, :], list_now[:, h, t:t + 1], list_now[:, h, at:at + 1],
                                      ALU.is_equal, ALU.mult)
                dve.tensor_scalar(hot_row[:, k * D:(k + 1) * D], iota_mark[:, :], list_now[:, h, t:t + 1], None,
                                  ALU.is_equal).then_inc(s_row, 1)

            def add_tile(n10, k, word):
                at = 6 * (k % HALF) - 7
                off = word & (63 << 6 * (k % HALF))
                off = (off >> at) if at >= 0 else (off << -at)
                off = dve.snap(off, min_val=0, max_val=NB * D)
                dst_ap = block_sum[:, bass.ds(off, D)]
                dve.wait_ge(s_sum, n10 + (1 + TILE_U - HALF))
                dve.wait_ge(s_acc, n10 + 1)
                dve.tensor_tensor(dst_ap, tile_sum(k), dst_ap, ALU.add).then_inc(s_acc, 1)

            def word_at(part):
                return dve.value_load(block_words[0:1, bass.ds(part, 1)], min_val=0, max_val=(1 << 30) - 1)

            def tiles(n, between=None, sort_pass=None):
                n10 = dve.snap(n * TILE_U)
                for k in range(TILE_U):
                    if k % HALF == 0:
                        word = word_at(n * 2 + (1 + k // HALF))
                    add_tile(n10 + k, (k + HALF) % TILE_U, word)
                    hots_tile(n, k)
                    if sort_pass is not None:
                        if k % SRC_H == 0:
                            dve.wait_ge(s_src, sort_pass * 2 + (1 + k // SRC_H))
                        hots_src(sort_pass * SRC_U + k, k)
                    if between is not None:
                        between(k)
                    for h, at in ((1, STAGE_AT[0]), (0, STAGE_AT[1])):
                        if k == at:
                            stage_list(h, n * 2 + (2 - h))
                            if sort_pass is not None:
                                stage_src(h, sort_pass * 2 + (2 - h))

            dve.tensor_copy(src_now[:, 0, :, :].rearrange("p r j -> p (r j)"), rec_flat[:, 0:PART]).then_inc(s_src, 1)
            with dve.Fori(0, SRC_G // SORT_C) as i:
                for c in range(SORT_C):
                    half = c // SRC_H
                    if c % SRC_H == 0:
                        dve.wait_ge(s_src, i * (SORT_C // SRC_H) + (half + 1))
                    hots_src(i * SORT_C + c, c % SRC_U)
                    if c % SRC_H == 1:
                        stage_src((half + 1) % 2, i * (SORT_C // SRC_H) + (half + 1))
            read_records(0)
            copy_types(0)
            for q in range(4):
                hots_types(0, q)
            dve.wait_ge(s_clear, 1)
            dve.wait_ge(s_w, 4)
            dve.tensor_copy(list_now[:, 0, :], list_flat[:, 0:LIST]).then_inc(s_list, 1)
            with dve.Fori(0, GROUPS - 1) as g:
                with dve.Fori(0, SORTING // 2) as i:
                    for half in range(2):
                        tiles(g * BODIES + (i * 2 + half), sort_pass=g * SORTING + (i * 2 + (half + SORTING)))

                for late in range(BODIES - SORTING):
                    def between(k):
                        t = late * TILE_U + k
                        if t == READ_AT:
                            read_records(g + 1)
                        if t == COPY_AT:
                            copy_types(g + 1)
                        if t + 1 in WEIGH_AT:
                            hots_types(g + 1, WEIGH_AT.index(t + 1))
                        if late == BODIES - SORTING - 1 and k == STAGE_AT[1]:
                            dve.wait_ge(s_w, g * 4 + 8)

                    tiles(g * BODIES + (SORTING + late), between)
            with dve.Fori((GROUPS - 1) * BODIES, GROUPS * BODIES) as i:
                tiles(i)
            word = word_at(2 * GROUPS * BODIES + 1)
            for k in range(HALF):
                add_tile(GROUPS * TILES + k, HALF + k, word)
            dve.drain()

            for c in range(NB // CH + 2):
                if c < NB // CH:
                    for j in range(c * CH, (c + 1) * CH):
                        dve.scalar_tensor_tensor(x_sb[:, j, :], block_sum[:, j * D:(j + 1) * D], small[:, 7, j:j + 1],
                                                 x_sb[:, j, :], ALU.mult, ALU.add, accum_out=stat[:, 2, j:j + 1])
                    dve.drain()
                    dve.tensor_scalar(stat[:, 2, chunk(c)], stat[:, 2, chunk(c)], -1.0 / D, None, ALU.mult)
                    dve.drain().then_inc(s_fin, 1)
                if c >= 2:
                    o = chunk(c - 2)
                    dve.wait_ge(s_std, c - 1)
                    dve.reciprocal(stat[:, 3, o], stat[:, 1, o])
                    dve.drain()
                    dve.tensor_tensor(stat[:, 4, o], stat[:, 2, o], stat[:, 3, o], ALU.mult)
                    dve.drain().then_inc(s_scale, 1)
                    for j in range(o.start, o.start + CH_DVE):
                        last = dve.tensor_scalar(x_sb[:, j, :], x_sb[:, j, :], stat[:, 2, j:j + 1], stat[:, 3, j:j + 1],
                                                 ALU.add, ALU.mult)
                    last.then_inc(s_outdve, 1)


def kernel(x, src, dst, edge_type_50, L0_gnn_bases, L0_gnn_comps, L0_gnn_alpha):
    import numpy as np
    import concourse.bacc as bacc
    from concourse.bass_utils import run_bass_kernel_spmd

    given = dict(x=x, src=src, dst=dst, etype=edge_type_50, bases=L0_gnn_bases, comps=L0_gnn_comps, alpha=L0_gnn_alpha)
    arrays = {name: np.ascontiguousarray(a) for name, a in given.items()}
    nc = bacc.Bacc("TRN2", target_bir_lowering=False, num_devices=1)
    aps = {name: nc.dram_tensor(name, a.shape, mybir.dt.from_np(a.dtype), kind="ExternalInput").ap()
           for name, a in arrays.items()}
    out = nc.dram_tensor("out", arrays["x"].shape, F32, kind="ExternalOutput").ap()
    relational_layer(nc, **aps, out=out)
    r = run_bass_kernel_spmd(nc, [arrays], core_ids=[0])
    return r.results[0]["out"]
```
